# Optimizing a Trainium2 kernel written in Bass

```python
import numpy as np
import jax
import jax.numpy as jnp

def _softmax(x, axis=-1):
    return jax.nn.softmax(x, axis=axis)

def _gelu(x):
    return jax.nn.gelu(x, approximate=True)

def _silu(x):
    return jax.nn.silu(x)

def _sigmoid(x):
    return jax.nn.sigmoid(x)

def _layernorm(x, axis=-1, eps=1e-05):
    m = jnp.mean(x, axis=axis, keepdims=True)
    v = jnp.var(x, axis=axis, keepdims=True)
    return (x - m) / jnp.sqrt(v + eps)

def _scatter_add(tgt, idx, src, axis=0):
    return tgt.at[idx].add(src)

def _segment_sum(src, seg, n):
    return jax.ops.segment_sum(src, seg, n)
kernel_name = 'mk_recurrent_d2_jaxref_r8_f5a789'

def setup_inputs(seed: int=0):
    np.random.seed(seed)
    _w = jnp.asarray

    def _L0_attn_setup():
        import jax, jax.numpy as jnp
        import numpy as np
        H = 128
        I = 256
        N = 16
        K = 4
        R = 64
        B = 2
        L = 512
        key = jax.random.key(seed)
        ks = jax.random.split(key, 10)
        hidden_states = jax.random.normal(ks[0], (B, L, H), dtype=jnp.float32)
        in_proj_w = jax.random.normal(ks[1], (2 * I, H), dtype=jnp.float32) * H ** (-0.5)
        conv_w = jax.random.normal(ks[2], (I, K), dtype=jnp.float32) * K ** (-0.5)
        conv_b = jax.random.normal(ks[3], (I,), dtype=jnp.float32) * 0.02
        x_proj_w = jax.random.normal(ks[4], (R + 2 * N, I), dtype=jnp.float32) * I ** (-0.5)
        dt_init_std = R ** (-0.5)
        dt_proj_w = jax.random.uniform(ks[5], (I, R), dtype=jnp.float32, minval=-dt_init_std, maxval=dt_init_std)
        dt = jnp.exp(jax.random.uniform(ks[6], (I,), dtype=jnp.float32) * (np.log(0.1) - np.log(0.001)) + np.log(0.001))
        dt = jnp.clip(dt, 0.0001)
        dt_proj_b = dt + jnp.log(-jnp.expm1(-dt))
        A_log = jnp.log(jnp.broadcast_to(jnp.arange(1, N + 1, dtype=jnp.float32)[None, :], (I, N)))
        D = jnp.ones((I,), dtype=jnp.float32)
        out_proj_w = jax.random.normal(ks[7], (H, I), dtype=jnp.float32) * I ** (-0.5)
        return {'hidden_states': hidden_states, 'in_proj_w': in_proj_w, 'conv_w': conv_w, 'conv_b': conv_b, 'x_proj_w': x_proj_w, 'dt_proj_w': dt_proj_w, 'dt_proj_b': dt_proj_b, 'A_log': A_log, 'D': D, 'out_proj_w': out_proj_w}
    _L0_attn_in = _L0_attn_setup()

    def _L0_ffn_setup():
        import jax, jax.numpy as jnp
        import numpy as np
        DMODEL = 128
        N_EXPERTS = 16
        EXPERT_SIZE = 32
        K = 4
        key = jax.random.key(seed)
        k1, k2, k3, k4 = jax.random.split(key, 4)
        std_sel = 1.0 / np.sqrt(DMODEL)
        std_val = 1.0 / np.sqrt(N_EXPERTS * EXPERT_SIZE)
        return {'x': jax.random.normal(k1, (4, 256, DMODEL), dtype=jnp.float32), 'expert_sel': jax.random.normal(k2, (N_EXPERTS, DMODEL), dtype=jnp.float32) * std_sel, 'keys': jax.random.normal(k3, (N_EXPERTS, DMODEL, EXPERT_SIZE), dtype=jnp.float32) * std_sel, 'values': jax.random.normal(k4, (N_EXPERTS, EXPERT_SIZE, DMODEL), dtype=jnp.float32) * std_val, 'route_scale': jnp.ones((1,), dtype=jnp.float32)}
    _L0_ffn_in = _L0_ffn_setup()

    def _L1_attn_setup():
        import jax, jax.numpy as jnp
        from jax import lax
        import numpy as np
        D_MODEL, D_STATE, EXPAND, D_CONV = (128, 16, 2, 4)
        D_INNER = EXPAND * D_MODEL
        B, L = (4, 256)

        def _ssm(xl, W_delta, b_delta, W_B, W_C, A_log):
            b, l, d_inner = xl.shape
            A = -jax.nn.softplus(A_log)
            delta = jnp.clip(jax.nn.softplus(xl @ W_delta.T + b_delta), 0.0001, 10.0)
            Bm = xl @ W_B.T
            Cm = xl @ W_C.T

            def step(h, inp):
                d_t, x_t, B_t, C_t = inp
                A_bar = jnp.exp(d_t[:, :, None] * A)
                h = A_bar * h + (d_t * x_t)[:, :, None] * B_t[:, None, :]
                y_t = jnp.einsum('bdn,bn->bd', h, C_t)
                return (h, y_t)
            h0 = jnp.zeros((b, d_inner, A_log.shape[0]), xl.dtype)
            xs = (jnp.swapaxes(delta, 0, 1), jnp.swapaxes(xl, 0, 1), jnp.swapaxes(Bm, 0, 1), jnp.swapaxes(Cm, 0, 1))
            _, ys = lax.scan(step, h0, xs)
            return jnp.swapaxes(ys, 0, 1)
        key = jax.random.key(seed)
        ks = jax.random.split(key, 12)

        def xavier(k, shape):
            fan_in, fan_out = (shape[1], shape[0])
            lim = float(np.sqrt(6.0 / (fan_in + fan_out)))
            return jax.random.uniform(k, shape, jnp.float32, -lim, lim)
        inp = {}
        inp['x'] = jax.random.normal(ks[0], (B, L, D_MODEL), jnp.float32)
        inp['W_left'] = xavier(ks[1], (D_INNER, D_MODEL))
        inp['conv_w'] = jax.random.normal(ks[2], (D_INNER, 1, D_CONV), jnp.float32) * (1.0 / np.sqrt(D_CONV))
        inp['conv_b'] = jax.random.normal(ks[3], (D_INNER,), jnp.float32) * 0.01
        inp['W_delta'] = jax.random.normal(ks[4], (D_INNER, D_INNER), jnp.float32) * (1.0 / np.sqrt(D_INNER))
        inp['b_delta'] = jnp.zeros((D_INNER,), jnp.float32)
        inp['W_B'] = jax.random.normal(ks[5], (D_STATE, D_INNER), jnp.float32) * (1.0 / np.sqrt(D_INNER))
        inp['W_C'] = jax.random.normal(ks[6], (D_STATE, D_INNER), jnp.float32) * (1.0 / np.sqrt(D_INNER))
        inp['A_log'] = jnp.log(jnp.arange(1, D_STATE + 1, dtype=jnp.float32))
        inp['W_right'] = xavier(ks[7], (D_INNER, D_MODEL))
        inp['ln_g'] = jnp.ones((D_INNER,), jnp.float32)
        inp['ln_b'] = jnp.zeros((D_INNER,), jnp.float32)
        inp['W_out'] = xavier(ks[8], (D_MODEL, D_INNER))
        return inp
    _L1_attn_in = _L1_attn_setup()

    def _L1_ffn_setup():
        import jax, jax.numpy as jnp
        import numpy as np
        D_MODEL = 128
        D_FF = 512
        NUM_EXPERTS = 8
        key = jax.random.key(seed)
        ks = jax.random.split(key, 8)
        scale_in = 1.0 / np.sqrt(D_MODEL)
        scale_ff = 1.0 / np.sqrt(D_FF)
        x = jax.random.normal(ks[0], (4, 256, D_MODEL), dtype=jnp.float32)
        gate_w = jax.random.uniform(ks[1], (NUM_EXPERTS, D_MODEL), jnp.float32, -scale_in, scale_in)
        gate_b = jax.random.uniform(ks[2], (NUM_EXPERTS,), jnp.float32, -scale_in, scale_in)
        expert_bias = jnp.zeros((NUM_EXPERTS,), dtype=jnp.float32)
        w1 = jax.random.uniform(ks[3], (NUM_EXPERTS, D_MODEL, D_FF), jnp.float32, -scale_in, scale_in)
        b1 = jax.random.uniform(ks[4], (NUM_EXPERTS, D_FF), jnp.float32, -scale_in, scale_in)
        w2 = jax.random.uniform(ks[5], (NUM_EXPERTS, D_FF, D_MODEL), jnp.float32, -scale_ff, scale_ff)
        b2 = jax.random.uniform(ks[6], (NUM_EXPERTS, D_MODEL), jnp.float32, -scale_ff, scale_ff)
        return {'x': x, 'gate_w': gate_w, 'gate_b': gate_b, 'expert_bias': expert_bias, 'w1': w1, 'b1': b1, 'w2': w2, 'b2': b2}
    _L1_ffn_in = _L1_ffn_setup()
    _d = {'L0_attn_hidden_states': _L0_attn_in['hidden_states'], 'L0_attn_in_proj_w': _L0_attn_in['in_proj_w'], 'L0_attn_conv_w': _L0_attn_in['conv_w'], 'L0_attn_conv_b': _L0_attn_in['conv_b'], 'L0_attn_x_proj_w': _L0_attn_in['x_proj_w'], 'L0_attn_dt_proj_w': _L0_attn_in['dt_proj_w'], 'L0_attn_dt_proj_b': _L0_attn_in['dt_proj_b'], 'L0_attn_A_log': _L0_attn_in['A_log'], 'L0_attn_D': _L0_attn_in['D'], 'L0_attn_out_proj_w': _L0_attn_in['out_proj_w'], 'L0_ffn_expert_sel': _L0_ffn_in['expert_sel'], 'L0_ffn_keys': _L0_ffn_in['keys'], 'L0_ffn_values': _L0_ffn_in['values'], 'L0_ffn_route_scale': _L0_ffn_in['route_scale'], 'L1_attn_W_left': _L1_attn_in['W_left'], 'L1_attn_conv_w': _L1_attn_in['conv_w'], 'L1_attn_conv_b': _L1_attn_in['conv_b'], 'L1_attn_W_delta': _L1_attn_in['W_delta'], 'L1_attn_b_delta': _L1_attn_in['b_delta'], 'L1_attn_W_B': _L1_attn_in['W_B'], 'L1_attn_W_C': _L1_attn_in['W_C'], 'L1_attn_A_log': _L1_attn_in['A_log'], 'L1_attn_W_right': _L1_attn_in['W_right'], 'L1_attn_ln_g': _L1_attn_in['ln_g'], 'L1_attn_ln_b': _L1_attn_in['ln_b'], 'L1_attn_W_out': _L1_attn_in['W_out'], 'L1_ffn_gate_w': _L1_ffn_in['gate_w'], 'L1_ffn_gate_b': _L1_ffn_in['gate_b'], 'L1_ffn_expert_bias': _L1_ffn_in['expert_bias'], 'L1_ffn_w1': _L1_ffn_in['w1'], 'L1_ffn_b1': _L1_ffn_in['b1'], 'L1_ffn_w2': _L1_ffn_in['w2'], 'L1_ffn_b2': _L1_ffn_in['b2']}
    _x0 = _d['L0_attn_hidden_states']
    _d['L0_attn_hidden_states'] = jax.random.normal(jax.random.fold_in(jax.random.key(seed), 1), (8, 1024, 128), dtype=_x0.dtype)
    del _x0
    return _d

def reference(L0_attn_hidden_states, L0_attn_in_proj_w, L0_attn_conv_w, L0_attn_conv_b, L0_attn_x_proj_w, L0_attn_dt_proj_w, L0_attn_dt_proj_b, L0_attn_A_log, L0_attn_D, L0_attn_out_proj_w, L0_ffn_expert_sel, L0_ffn_keys, L0_ffn_values, L0_ffn_route_scale, L1_attn_W_left, L1_attn_conv_w, L1_attn_conv_b, L1_attn_W_delta, L1_attn_b_delta, L1_attn_W_B, L1_attn_W_C, L1_attn_A_log, L1_attn_W_right, L1_attn_ln_g, L1_attn_ln_b, L1_attn_W_out, L1_ffn_gate_w, L1_ffn_gate_b, L1_ffn_expert_bias, L1_ffn_w1, L1_ffn_b1, L1_ffn_w2, L1_ffn_b2):

    def _L0_attn_ref(hidden_states, in_proj_w, conv_w, conv_b, x_proj_w, dt_proj_w, dt_proj_b, A_log, D, out_proj_w):
        import jax, jax.numpy as jnp
        import numpy as np
        H = 128
        I = 256
        N = 16
        K = 4
        R = 64
        B = 2
        L = 512
        proj = jnp.einsum('blh,ph->blp', hidden_states, in_proj_w)
        x, gate = jnp.split(proj, 2, axis=-1)
        xc = x.transpose(0, 2, 1)
        kernel = conv_w[:, None, :]
        xc = jax.lax.conv_general_dilated(xc, kernel, window_strides=(1,), padding=[(K - 1, 0)], dimension_numbers=('NCH', 'OIH', 'NCH'), feature_group_count=I)
        xc = jax.nn.silu(xc + conv_b[None, :, None])
        xl = xc.transpose(0, 2, 1)
        ssm = jnp.einsum('bli,pi->blp', xl, x_proj_w)
        dt_low, Bm, Cm = jnp.split(ssm, [R, R + N], axis=-1)
        dt = jnp.einsum('blr,ir->bli', dt_low, dt_proj_w) + dt_proj_b
        dt = jax.nn.softplus(dt)
        A = -jnp.exp(A_log)

        def step(h, inp):
            x_t, dt_t, B_t, C_t = inp
            dA = jnp.exp(dt_t[:, :, None] * A[None])
            h = h * dA + dt_t[:, :, None] * B_t[:, None, :] * x_t[:, :, None]
            y = jnp.einsum('bin,bn->bi', h, C_t)
            return (h, y)
        h0 = jnp.zeros((xl.shape[0], I, N), xl.dtype)
        xs = (xl.transpose(1, 0, 2), dt.transpose(1, 0, 2), Bm.transpose(1, 0, 2), Cm.transpose(1, 0, 2))
        _, ys = jax.lax.scan(step, h0, xs)
        y = ys.transpose(1, 0, 2) + xl * D[None, None, :]
        y = y * jax.nn.silu(gate)
        return jnp.einsum('bli,hi->blh', y, out_proj_w)

    def _L0_ffn_ref(x, expert_sel, keys, values, route_scale):
        import jax, jax.numpy as jnp
        import numpy as np
        DMODEL = 128
        N_EXPERTS = 16
        EXPERT_SIZE = 32
        K = 4
        sel_logits = jnp.einsum('btd,ed->bte', x, expert_sel)
        sel_probs = jax.nn.sigmoid(sel_logits)
        _, sel_index = jax.lax.top_k(sel_probs, K)
        sel_val = jnp.take_along_axis(sel_probs, sel_index, axis=-1)
        sel_val = sel_val / jnp.clip(sel_val.sum(-1, keepdims=True), 1e-09)
        sel_val = sel_val * route_scale
        scores_all = jax.nn.relu(jnp.einsum('btd,edh->bteh', x, keys))
        values_all = jnp.einsum('bteh,ehv->btev', scores_all, values)
        sel_idx_exp = sel_index[..., None]
        selected = jnp.take_along_axis(values_all, sel_idx_exp, axis=2)
        out = (selected * sel_val[..., None]).sum(axis=2)
        return out

    def _L1_attn_ref(x, W_left, conv_w, conv_b, W_delta, b_delta, W_B, W_C, A_log, W_right, ln_g, ln_b, W_out):
        import jax, jax.numpy as jnp
        from jax import lax
        import numpy as np
        D_MODEL, D_STATE, EXPAND, D_CONV = (128, 16, 2, 4)
        D_INNER = EXPAND * D_MODEL
        B, L = (4, 256)

        def _ssm(xl, W_delta, b_delta, W_B, W_C, A_log):
            b, l, d_inner = xl.shape
            A = -jax.nn.softplus(A_log)
            delta = jnp.clip(jax.nn.softplus(xl @ W_delta.T + b_delta), 0.0001, 10.0)
            Bm = xl @ W_B.T
            Cm = xl @ W_C.T

            def step(h, inp):
                d_t, x_t, B_t, C_t = inp
                A_bar = jnp.exp(d_t[:, :, None] * A)
                h = A_bar * h + (d_t * x_t)[:, :, None] * B_t[:, None, :]
                y_t = jnp.einsum('bdn,bn->bd', h, C_t)
                return (h, y_t)
            h0 = jnp.zeros((b, d_inner, A_log.shape[0]), xl.dtype)
            xs = (jnp.swapaxes(delta, 0, 1), jnp.swapaxes(xl, 0, 1), jnp.swapaxes(Bm, 0, 1), jnp.swapaxes(Cm, 0, 1))
            _, ys = lax.scan(step, h0, xs)
            return jnp.swapaxes(ys, 0, 1)
        d_conv = conv_w.shape[-1]
        left = x @ W_left.T
        left_ncw = jnp.swapaxes(left, 1, 2)
        left_ncw = jnp.pad(left_ncw, ((0, 0), (0, 0), (d_conv - 1, 0)))
        left_ncw = lax.conv_general_dilated(left_ncw, conv_w, window_strides=(1,), padding='VALID', feature_group_count=conv_w.shape[0]) + conv_b[None, :, None]
        left = jax.nn.silu(jnp.swapaxes(left_ncw, 1, 2))
        ssm_out = _ssm(left, W_delta, b_delta, W_B, W_C, A_log)
        gate = jax.nn.silu(x @ W_right.T)
        out = ssm_out * gate
        mu = jnp.mean(out, axis=-1, keepdims=True)
        var = jnp.mean(jnp.square(out - mu), axis=-1, keepdims=True)
        out = (out - mu) * lax.rsqrt(var + 1e-05) * ln_g + ln_b
        return out @ W_out.T

    def _L1_ffn_ref(x, gate_w, gate_b, expert_bias, w1, b1, w2, b2):
        import jax, jax.numpy as jnp
        import numpy as np
        D_MODEL = 128
        D_FF = 512
        NUM_EXPERTS = 8
        gate_logits = jnp.einsum('bsd,ed->bse', x, gate_w) + gate_b + expert_bias
        top_idx = jnp.argmax(gate_logits, axis=-1)
        out = jnp.zeros_like(x)
        for e in range(NUM_EXPERTS):
            mask = (top_idx == e)[..., None].astype(x.dtype)
            h = jax.nn.relu(jnp.einsum('bsd,df->bsf', x, w1[e]) + b1[e])
            y = jnp.einsum('bsf,fd->bsd', h, w2[e]) + b2[e]
            out = out + mask * y
        return out
    x = L0_attn_hidden_states
    xn = _layernorm(x, axis=-1)
    s = _L0_attn_ref(xn, L0_attn_in_proj_w, L0_attn_conv_w, L0_attn_conv_b, L0_attn_x_proj_w, L0_attn_dt_proj_w, L0_attn_dt_proj_b, L0_attn_A_log, L0_attn_D, L0_attn_out_proj_w)
    g = _silu(_L0_ffn_ref(xn, L0_ffn_expert_sel, L0_ffn_keys, L0_ffn_values, L0_ffn_route_scale))
    x = x + s * g
    xn = _layernorm(x, axis=-1)
    s = _L1_attn_ref(xn, L1_attn_W_left, L1_attn_conv_w, L1_attn_conv_b, L1_attn_W_delta, L1_attn_b_delta, L1_attn_W_B, L1_attn_W_C, L1_attn_A_log, L1_attn_W_right, L1_attn_ln_g, L1_attn_ln_b, L1_attn_W_out)
    g = _silu(_L1_ffn_ref(xn, L1_ffn_gate_w, L1_ffn_gate_b, L1_ffn_expert_bias, L1_ffn_w1, L1_ffn_b1, L1_ffn_w2, L1_ffn_b2))
    x = x + s * g
    return x

_drawn_inputs = setup_inputs


def setup_inputs(seed=0):
    import zlib

    import numpy as np

    out = dict(_drawn_inputs(seed))
    spreads = {'L0_attn_D': (1.0, 0.6),
     'L1_attn_b_delta': (0.0, 2.0),
     'L1_attn_ln_g': (1.0, 0.6),
     'L1_attn_ln_b': (0.0, 2.0),
     'L1_ffn_expert_bias': (0.0, 0.8)}
    factors = {'L0_attn_conv_b': 8.0,
     'L0_attn_x_proj_w': 7.719,
     'L0_attn_dt_proj_w': 8.0,
     'L0_attn_dt_proj_b': 8.0,
     'L0_attn_A_log': 8.0,
     'L1_attn_conv_b': 64.0,
     'L1_ffn_b1': 36.264,
     'L1_ffn_b2': 29.312,
     'L1_attn_W_left': 6.025,
     'L1_attn_conv_w': 5.817,
     'L1_attn_W_delta': 8.0,
     'L1_attn_W_B': 5.986,
     'L1_attn_W_C': 5.898,
     'L1_attn_A_log': 8.0,
     'L1_attn_W_right': 6.311,
     'L1_attn_W_out': 5.384,
     'L1_ffn_gate_w': 5.888,
     'L1_ffn_gate_b': 8.0,
     'L1_ffn_w1': 7.489,
     'L1_ffn_w2': 5.899}
    for name, (base, spread) in spreads.items():
        noise = np.random.default_rng([zlib.crc32(name.encode()), seed]).standard_normal(out[name].shape)
        drawn = base * np.exp(spread * noise) if base else spread * noise
        out[name] = jnp.asarray(drawn.astype(out[name].dtype))
    for name, factor in factors.items():
        out[name] = (out[name] * factor).astype(out[name].dtype)
    return out
```

```python
from contextlib import ExitStack

import concourse.bass as bass
from concourse import mybir

ALU = mybir.AluOpType
ACT = mybir.ActivationFunctionType
AX = mybir.AxisListType
F32 = mybir.dt.float32
I32 = mybir.dt.int32
BF16 = mybir.dt.bfloat16
EXP_LN = "natural_log_exp_and_others"

P = 128
SEQS, LEN, DM = 8, 1024, 128
CH = 2
HALF = LEN // 2
TILES = LEN // P
NS = 16
UNITS = 2 * NS
TAPS = 4
RANK = 64
E0, K0, EH = 16, 4, 32
E1, FF = 8, 512
FB = FF // P
BLOCKS = LEN // P + E1 - 1
R_LAG = 4
SENTINEL = 3.0e38
EPS = 1e-5
LN_ERROR = 4e-9


def at_least(eng, sem, value):
    if isinstance(value, int) and value <= 0:
        return
    eng.wait_ge(sem, value)


def build(nc, T, out):
    ctx = ExitStack()
    with ctx:
        def sb(name, shape, dt=F32):
            return ctx.enter_context(nc.sbuf_tensor(name, shape, dt))

        def pb(name):
            return ctx.enter_context(nc.psum_tensor(name, [P, 512], F32))

        def sem(name):
            return ctx.enter_context(nc.semaphore(name))

        x1_dram = T["x1"]

        ident = sb("ident", [P, P])
        part_rows = sb("part_rows", [96, 2 * NS])
        spread = sb("spread", [96, 2 * NS, P], BF16)
        in_w = sb("in_w", [P, 4 * P])
        conv_w = [sb(f"conv_w{l}", [P, CH, TAPS]) for l in range(2)]
        conv_b = [sb(f"conv_b{l}", [P, CH]) for l in range(2)]
        x_w = sb("x_w", [P, CH, RANK + 2 * NS])
        dt_w = sb("dt_w", [RANK, CH * P])
        dt_b = [sb(f"dt_b{l}", [P, CH]) for l in range(2)]
        A = [sb(f"A{l}", [P, CH, NS]) for l in range(2)]
        skip_d = sb("skip_d", [P, CH])
        out_w = [sb(f"out_w{l}", [P, CH, DM]) for l in range(2)]
        sel_w = sb("sel_w", [P, E0])
        keys = sb("keys", [P, E0 * EH])
        values = sb("values", [P, 4, DM])
        route = sb("route", [P, 1])
        delta_w = sb("delta_w", [P, CH, CH * P])
        side_w = sb("side_w", [P, 4 * P])
        bc_w = sb("bc_w", [P, CH, 2 * NS])
        ln_g = sb("ln_g", [P, CH])
        ln_b = sb("ln_b", [P, CH])
        gain_sum = sb("gain_sum", [P, DM])
        bias_out = sb("bias_out", [P, DM])
        gate_w = sb("gate_w", [P, E1])
        gate_b = sb("gate_b", [P, E1])
        expert_bias = sb("expert_bias", [P, E1])
        before = sb("before", [P, P], BF16)
        ones = sb("ones", [P, P], BF16)
        tile_sizes = sb("tile_sizes", [P, E1, E1])
        tile_numbers = sb("tile_numbers", [P, BLOCKS, E1])
        idle = sb("idle", [P, 2])
        small = sb("small", [P, 4, 2 * NS])

        x_tok = sb("x_tok", [P, TILES, DM])
        x_back = sb("x_back", [P, TILES, DM])
        g_tok = [sb(f"g_tok{q}", [P, TILES, DM]) for q in range(2)]
        stats = sb("stats", [P, TILES, 6])
        mv = sb("mv", [P, TILES, 2])
        rstd = sb("rstd", [P, TILES])
        xnT = sb("xnT", [P, LEN])
        conv_in = sb("conv_in", [P, CH, LEN + TAPS])
        xl = [sb(f"xl{q}", [P, CH, LEN]) for q in range(2)]
        zs = [sb(f"zs{q}", [P, CH, LEN]) for q in range(2)]
        dt = [sb(f"dt{q}", [P, CH, LEN]) for q in range(2)]
        u = [sb(f"u{q}", [P, CH, LEN]) for q in range(2)]
        sp_z0 = sb("sp_z", [P, LEN])
        sp_e0 = sb("sp_e", [P, LEN])
        sp_l0 = sb("sp_l", [P, LEN])
        xn = sp_z0[:, :].rearrange("p (j d) -> p j d", d=DM)
        dt_low = sb("dt_low", [RANK, LEN])
        parts = [sb(f"parts{q}", [96, LEN], BF16) for q in range(2)]
        rest = [u[q][0:2 * NS, 0, :] for q in range(2)]
        mid = [u[q][0:2 * NS, 1, 0:HALF].bitcast(BF16) for q in range(2)]
        probs = sb("probs", [P, TILES, 24])
        replaced = sb("replaced", [P, TILES, 24])
        top = sb("top", [P, TILES, 8])
        wanted = sb("wanted", [P, TILES, 16])
        share = sb("share", [P, TILES, E0])
        share_sum = sb("share_sum", [P, TILES])
        ffn = sb("ffn", [P, 4, 512])
        scored = [ffn[:, j, :] for j in range(2)]
        scoredT = [ffn[:, 2 + j, :] for j in range(2)]
        sp_z = [sp_z0[:, :], ffn[:, 0:2, :].rearrange("p a b -> p (a b)")]
        sp_e = [sp_e0[:, :], ffn[:, 2:4, :].rearrange("p a b -> p (a b)")]
        sp_l = [sp_l0[:, :], x_tok[:, :, :].rearrange("p a b -> p (a b)")]
        sp_q = [conv_in[:, c, TAPS:TAPS + LEN] for c in range(CH)]
        expert = [sb(f"expert{j}", [P, 2 * FF + FB + DM]) for j in range(2)]
        block_x = [sb(f"block_x{j}", [P, DM]) for j in range(2)]
        block_xT = [sb(f"block_xT{j}", [P, P]) for j in range(2)]
        hidden = [keys, values[:, :, :].rearrange("p a b -> p (a b)")]
        block_y = [sb(f"block_y{j}", [P, DM]) for j in range(2)]
        onehot = sb("onehot", [P, TILES, E1], BF16)
        marks = sb("marks", [P, BLOCKS, E1])
        ones_e = sb("ones_e", [P, E1])
        zeros = block_y[0]
        blocks_of = sb("blocks_of", [P, E1])
        block_end = sb("block_end", [P, E1])
        first_slot = sb("first_slot", [P, E1])
        place = sb("place", [P, TILES, E1])
        place_sum = sb("place_sum", [P, TILES])
        expert_f = sb("expert_f", [P, BLOCKS])
        slot_of = [sb(f"slot_of{j}", [P, TILES], I32) for j in range(2)]
        block_expert = [sb(f"block_expert{j}", [P, BLOCKS], I32) for j in range(2)]

        decay = [sb(f"decay{j}", [P, CH, HALF]) for j in range(2)]
        inject = [sb(f"inject{j}", [P, CH, HALF]) for j in range(2)]
        hs = [sb(f"hs{j}", [P, CH, HALF]) for j in range(2)]
        c_sb = [sb(f"c_sb{j}", [P, HALF]) for j in range(2)]
        weighted = [sb(f"weighted{j}", [P, CH, HALF]) for j in range(4)]
        carry = sb("carry", [P, NS, CH])
        one_col = hs[0][:, :, 0:P]
        sum_tok = sp_l0[:, :].rearrange("p (j d) -> p j d", d=DM)
        out_stats = sb("out_stats", [P, TILES, 6])
        out_mv = sb("out_mv", [P, TILES, 2])
        out_r = sb("out_r", [P, TILES])
        out_nm = sb("out_nm", [P, TILES])

        b_ps = [pb(f"b_ps{j}") for j in range(2)]
        c_ps = pb("c_ps")
        y_ps = [pb(f"y_ps{c}") for c in range(CH)]
        side_ps = [pb(f"side_ps{j}") for j in range(3)]

        loaded = sem("loaded")
        prep = sem("prep")
        prep_act = sem("prep_act")
        prep_pe = sem("prep_pe")
        x_in, x_back_in = sem("x_in"), sem("x_back_in")
        expert_in = [sem(f"expert_in{j}") for j in range(2)]
        block_in = [sem(f"block_in{j}") for j in range(2)]
        block_out = [sem(f"block_out{j}") for j in range(2)]
        place_step, expert_step = sem("place_step"), sem("expert_step")
        slot_step = sem("slot_step")
        slots_ready, experts_ready = sem("slots_ready"), sem("experts_ready")
        zeroed, scattered, gathered = sem("zeroed"), sem("scattered"), sem("gathered")
        stored = sem("stored")
        b_ready, c_ready = sem("b_ready"), sem("c_ready")
        c_copied = sem("c_copied")
        decay_ready = sem("decay_ready")
        inject_ready = sem("inject_ready")
        scanned = sem("scanned")
        carried = sem("carried")
        weighted_ready = sem("weighted_ready")
        summed = sem("summed")
        y_taken = sem("y_taken")
        evac = sem("evac")
        full = [sem(f"side_full{j}") for j in range(3)]
        free = [sem(f"side_free{j}") for j in range(3)]
        z_ready = sem("z_ready")
        back_sum = sem("back_sum")
        turned_stats = sem("turned_stats")
        ln_step = sem("ln_step")
        rstd_ready = sem("rstd_ready")
        conv_step = sem("conv_step")
        gate_step0, gate_step1 = sem("gate_step0"), sem("gate_step1")
        g_ready = sem("g_ready")
        silu_ready = sem("silu_ready")
        dt_low_ready = sem("dt_low_ready")
        hi_ready, mid_ready, mid_copied = sem("hi_ready"), sem("mid_ready"), sem("mid_copied")
        lo_ready = sem("lo_ready")
        sp_act, sp_dve = sem("sp_act"), sem("sp_dve")
        u_ready = sem("u_ready")
        back_step0, back_step1 = sem("back_step0"), sem("back_step1")
        back_act = sem("back_act")

        FRONT = [
            [(4, "tr0", 0), (4, "tr1", 1), (7, "x00", 0), (7, "x01", 1), (7, "logits", 2), (8, "x10", 0), (8, "x11", 1)]
            + [(10 + j, f"score{j}", 0) for j in range(TILES)] + [(11 + j, f"turn{j}", 1) for j in range(TILES)]
            + [(12, "values0", 2), (16, "values1", 2)],
            [(4, "tr0", 0), (4, "tr1", 1), (8, "x00", 0), (8, "x01", 1), (9, "logits", 2), (10, "x10", 0), (10, "x11", 1)] + [(12, "ranks", 0)],
        ]
        for U in FRONT:
            U += [(19, "z00", 0), (19, "z01", 1), (20, "z10", 0), (20, "z11", 1), (22, "proj0", 2), (22, "proj1", 0),
                  (24, "dt00", 1), (24, "dt01", 2), (26, "dt10", 0), (26, "dt11", 1)]
        BACK = [
            [(5, "out0", 2), (5, "out1", 0)],
            [(5, "turned0", 2), (5, "turned1", 0), (7, "turned2", 0), (7, "turned3", 2), (11, "out0", 2), (11, "out1", 0)],
        ]

        BLOCK = []
        for i in range(BLOCKS):
            BLOCK += [(2 * i, 2, f"T{i}", 2 if 2 * i == 20 else 1), (2 * i + 1, 2, f"H{i}", 1),
                      (2 * i + 2, 2, f"Y{i}", 1 if 2 * i + 2 == 22 else 2)]

        def layer_at(seq):
            return None if seq < 0 or seq >= 2 * SEQS else int(seq >= SEQS)

        def uses(like):
            b, f = layer_at(like - 1), layer_at(like + 1)
            U = [(k, 0, n, j) for k, n, j in (BACK[b] if b is not None else [])] \
                + [(k, 1, n, j) for k, n, j in (FRONT[f] if f is not None else [])]
            U += BLOCK if layer_at(like) == 1 else []
            return [(n, j) for k, _, n, j in sorted(U, key=lambda v: (v[0], v[1], v[1] == 2 and v[2][0] == "T"))]

        BANKS = {like: [[n for n, b in uses(like) if b == j] for j in range(3)] for like in range(-1, 2 * SEQS + 1)}
        BEFORE = {like: [sum(len(BANKS[m][j]) for m in range(-1, like)) for j in range(3)] for like in BANKS}

        def use(B, name):
            g, like = B
            j = [j for j in range(3) if name in BANKS[like][j]][0]
            n = BEFORE[like][j] + BANKS[like][j].index(name) + 1
            return j, n + (0 if isinstance(g, int) else (g - like) * len(BANKS[like][j]))

        def fill(pe, B, name):
            j, count = use(B, name)
            at_least(pe, free[j], count - 1)
            return side_ps[j], full[j]

        def taken(eng, B, name):
            j, count = use(B, name)
            eng.wait_ge(free[j], count)

        def take(eng, B, name):
            j, count = use(B, name)
            eng.wait_ge(full[j], count)
            return side_ps[j], free[j]

        def wait_apart(dve, sem, value):
            dve.wait_ge(sem, value)
            dve.tensor_copy(idle[:, 1:2], idle[:, 0:1])

        block = ctx.enter_context(nc.Block())

        N_LOADS = 0
        plain = [(ident, "ident"), (part_rows, "part_rows"), (in_w, "in_w"), (conv_w[0], "conv_w0"),
                 (conv_w[1], "conv_w1"), (conv_b[0], "conv_b0"), (conv_b[1], "conv_b1"), (x_w, "x_w"),
                 (dt_w, "dt_w"), (dt_b[0], "dt_b0"), (dt_b[1], "dt_b1"), (A[0], "A_log0"), (skip_d, "skip_d"),
                 (out_w[0], "out_w0"), (out_w[1], "out_w1"), (sel_w, "sel_w"), (keys, "keys"), (values, "values"),
                 (delta_w, "delta_w"), (bc_w, "bc_w"), (ln_g, "ln_g"),
                 (ln_b, "ln_b"), (gate_w, "gate_w"), (before, "before"), (ones, "ones")]
        spreads = [(route, "route", 1), (gate_b, "gate_b", E1), (expert_bias, "expert_bias", E1)]
        N_LOADS = 16 * (len(plain) + len(spreads) + 1)
        N_LOADS += 16 * 3

        x_src = [T["x"], x1_dram]
        x_dst = [x1_dram, out]

        def rows(ap, s):
            return ap.rearrange("(s j p) d -> s p j d", s=SEQS, p=P)[bass.ds(s, 1)].rearrange("a p j d -> p (a j) d")

        LAST_BACK = 24

        def sp_load_x(sp, layer, s, g):
            at_least(sp, u_ready, g)
            sp.dma_start(x_tok[:, :, :], rows(x_src[layer], s)).then_inc(x_in, 16)

        def sp_back(sp, layer, s, g, k):
            if k == 1:
                sp.wait_ge(stored, 16 * (g + 2))
                sp.dma_start(x_back[:, :, :], rows(x_src[layer], s)).then_inc(x_back_in, 16)
            if k == (8, 24)[layer]:
                sp.wait_ge((back_step0, back_step1)[layer], (1, 5)[layer] * (s + 1))
                sp.dma_start(rows(x_dst[layer], s), x_back[:, :, :]).then_inc(stored, 16)
        PER_BODY = [(BLOCKS + 1) // 2, BLOCKS // 2]

        def block_count(s, i):
            return PER_BODY[i % 2] * s + i // 2 + 1

        def sp_load_block(sp, B, s, par, i):
            j = i % 2
            if i == 0:
                sp.wait_ge(scattered, 16 * TILES * (s + 1))
            sp.dma_start(block_x[j][:, :], T[f"sorted_x{par}"][i * P:(i + 1) * P, :]).then_inc(block_in[j], 16)
            e = sp.value_load(block_expert[par][0:1, i:i + 1], min_val=0, max_val=E1 - 1)
            sp.dma_start(expert[j][:, :], T["experts"][bass.ds(e, 1)].rearrange("a p n -> p (a n)"))\
                .then_inc(expert_in[j], 16)

        def sp_blocks(sp, B, s, par, k):
            i = k // 2
            if k % 2 == 0 and 1 <= i <= BLOCKS:
                taken(sp, B, f"Y{i - 1}")
                sp.dma_start(T[f"sorted_y{par}"][(i - 1) * P:i * P, :], block_y[(i - 1) % 2][:, :])\
                    .then_inc(block_out[(i - 1) % 2], 16)
            if k % 2 == 0 and i + 1 < BLOCKS:
                sp_load_block(sp, B, s, par, i + 1)

        def pe_blocks(pe, B, s, k):
            i = k // 2
            if k % 2 == 0:
                if 1 <= i <= BLOCKS:
                    n = i - 1
                    taken(pe, B, f"H{n}")
                    bank, done = fill(pe, B, f"Y{n}")
                    for m in range(FB):
                        mm = pe.matmul(bank[:, 0:DM], hidden[n % 2][:, m * P:(m + 1) * P],
                                       expert[n % 2][:, FF + m * DM:FF + (m + 1) * DM], start=(m == 0), stop=(m == FB - 1))
                    mm.then_inc(done, 1)
                if i < BLOCKS:
                    pe.wait_ge(block_in[i % 2], 16 * block_count(s, i))
                    bank, done = fill(pe, B, f"T{i}")
                    pe.transpose(bank[:, 0:P], block_x[i % 2][:, :], ident[:, :]).then_inc(done, 1)
            elif i < BLOCKS:
                pe.wait_ge(expert_in[i % 2], 16 * block_count(s, i))
                taken(pe, B, f"T{i}")
                bank, done = fill(pe, B, f"H{i}")
                for m in range(FB):
                    mm = pe.matmul(bank[:, m * P:(m + 1) * P], expert[i % 2][:, m * P:(m + 1) * P], block_xT[i % 2][:, :],
                                   start=True, stop=True)
                mm.then_inc(done, 1)

        def act_blocks(act, B, s, k):
            i = k // 2
            if i >= BLOCKS:
                return
            if k % 2 == 0:
                bank, done = take(act, B, f"T{i}")
                act.activation(block_xT[i % 2][:, :], bank[:, 0:P], ACT.Copy).then_inc(done, 1)
            else:
                if i >= 2:
                    take(act, B, f"Y{i - 2}")
                bank, done = take(act, B, f"H{i}")
                for m in range(FB):
                    a = act.activation(hidden[i % 2][:, m * P:(m + 1) * P], bank[:, m * P:(m + 1) * P], ACT.Relu,
                                       bias=expert[i % 2][:, 2 * FF + m:2 * FF + m + 1])
                a.then_inc(done, 1)

        def dve_blocks(dve, B, s, k):
            i = k // 2 - 1
            if k % 2 == 0 and 0 <= i < BLOCKS:
                at_least(dve, block_out[i % 2], 16 * (block_count(s, i) - 1))
                bank, done = take(dve, B, f"Y{i}")
                dve.tensor_tensor(block_y[i % 2][:, :], bank[:, 0:DM], expert[i % 2][:, 2 * FF + FB:2 * FF + FB + DM],
                                  ALU.add).then_inc(done, 1)

        S_SCATTER, B_GATHER = 16, 1

        def pool_waits(pool, front, back, k):
            if front is not None and k == S_SCATTER:
                s = front
                pool.wait_ge(experts_ready, s + 1)
                pool.wait_ge(zeroed, 16 * 2 * (BLOCKS - 1))
                for j in range(2):
                    at_least(pool, block_in[j], 16 * PER_BODY[j] * (s - 1))
            if back is not None and k == B_GATHER:
                for j in range(2):
                    pool.wait_ge(block_out[j], 16 * PER_BODY[j] * (back + 1))

        def pool_indirect(pool, front, back, par, k):
            if front is not None and S_SCATTER <= k < S_SCATTER + TILES // 2:
                for n in range(2):
                    j = 2 * (k - S_SCATTER) + n
                    pool.indirect_dma_start(T[f"sorted_x{par}"], bass.IndirectOffsetOnAxis(slot_of[par][:, j:j + 1], 0),
                                            xn[:, j, :], None).then_inc(scattered, 16)
            if back is not None and B_GATHER <= k < B_GATHER + TILES // 2:
                for n in range(2):
                    j = 2 * (k - B_GATHER) + n
                    pool.indirect_dma_start(g_tok[par][:, j, :], None, T[f"sorted_y{par}"],
                                            bass.IndirectOffsetOnAxis(slot_of[par][:, j:j + 1], 0)).then_inc(gathered, 16)

        S_LOAD, S_STATS, S_RSTD, S_NORM, S_TURN = 0, 1, 2, 3, 4
        S_CONV = (9, 12)
        S_GATE = (8, 10)
        S_FFN, S_Z, S_SILU, S_PROJ, S_SP, S_U = 10, 19, 21, 22, 24, 30

        def sp_front(sp, B, layer, s, g, q, k):
            if k == S_LOAD:
                sp_load_x(sp, layer, s, g)
            if layer == 1 and k == UNITS - 1:
                sp_load_block(sp, B, s, q, 0)

        def pe_front(pe, B, layer, s, g, q, k):
            if k == S_TURN:
                pe.wait_ge(ln_step, 3 * g + 3)
                for n in range(2):
                    bank, done = fill(pe, B, f"tr{n}")
                    for j in range(4):
                        mm = pe.transpose(bank[:, j * P:(j + 1) * P], xn[:, 4 * n + j, :], ident[:, :])
                    mm.then_inc(done, 1)
            w = in_w if layer == 0 else side_w
            for c in range(CH):
                if k == ((7, 8), (8, 10))[layer][c]:
                    if c == 0:
                        taken(pe, B, "tr0")
                        taken(pe, B, "tr1")
                    for t in range(2):
                        bank, done = fill(pe, B, f"x{c}{t}")
                        pe.matmul(bank[:, :], w[:, c * P:(c + 1) * P], xnT[:, t * HALF:(t + 1) * HALF],
                                  start=True, stop=True).then_inc(done, 1)
            if k == (7, 9)[layer]:
                bank, done = fill(pe, B, "logits")
                v, n = ((sel_w, E0), (gate_w, E1))[layer]
                for j in range(TILES):
                    mm = pe.matmul(bank[:, n * j:n * j + n], xnT[:, j * P:(j + 1) * P], v[:, :], start=True, stop=True)
                mm.then_inc(done, 1)
            if layer == 0:
                j = k - S_FFN
                if 0 <= j < TILES:
                    bank, done = fill(pe, B, f"score{j}")
                    pe.matmul(bank[:, :], xnT[:, j * P:(j + 1) * P], keys[:, :], start=True, stop=True).then_inc(done, 1)
                j = k - S_FFN - 1
                if 0 <= j < TILES:
                    taken(pe, B, f"score{j}")
                    bank, done = fill(pe, B, f"turn{j}")
                    for m in range(4):
                        mm = pe.transpose(bank[:, m * P:(m + 1) * P], scored[j % 2][:, m * P:(m + 1) * P], ident[:, :])
                    mm.then_inc(done, 1)
                j = k - S_FFN - 2
                if 0 <= j < TILES:
                    taken(pe, B, f"turn{j}")
                    if j % 4 == 0:
                        bank, done = fill(pe, B, f"values{j // 4}")
                    else:
                        bank, done = side_ps[2], full[2]
                    for m in range(4):
                        mm = pe.matmul(bank[:, (j % 4) * DM:(j % 4 + 1) * DM], scoredT[j % 2][:, m * P:(m + 1) * P],
                                       values[:, m, :], start=(m == 0), stop=(m == 3))
                    mm.then_inc(value_done if j % 4 < 3 else done, 1)
            if layer == 1 and k == 12:
                pe.wait_ge(gate_step1, 5 * s + 5)
                bank, done = fill(pe, B, "ranks")
                pe.matmul(bank[:, 0:TILES * E1], before[:, :], onehot[:, :, :].rearrange("p j e -> p (j e)"),
                          start=True, stop=False)
                for j in range(TILES - 1):
                    n = TILES - 1 - j
                    pe.matmul(bank[:, (j + 1) * E1:TILES * E1], ones[:, :],
                              onehot[:, j, :].unsqueeze(1).to_broadcast([P, n, E1]), start=False, stop=(n == 1))
                for j in range(TILES):
                    mm = pe.matmul(bank[:, TILES * E1:(TILES + 1) * E1], ones[:, :], onehot[:, j, :],
                                   start=(j == 0), stop=(j == TILES - 1))
                mm.then_inc(done, 1)
            if S_Z <= k < S_Z + CH:
                c = k - S_Z
                for t in range(2):
                    bank, done = fill(pe, B, f"z{c}{t}")
                    pe.matmul(bank[:, :], w[:, (CH + c) * P:(CH + c + 1) * P], xnT[:, t * HALF:(t + 1) * HALF],
                              start=True, stop=True).then_inc(done, 1)
            if k == S_PROJ:
                pe.wait_ge(silu_ready, g + 1)
                v, n = ((x_w, RANK + 2 * NS), (bc_w, 2 * NS))[layer]
                for t in range(2):
                    bank, done = fill(pe, B, f"proj{t}")
                    for c in range(CH):
                        mm = pe.matmul(bank[0:n, :], v[:, c, :], xl[q][:, c, t * HALF:(t + 1) * HALF],
                                       start=(c == 0), stop=(c == CH - 1))
                    mm.then_inc(done, 1)
            if k in (S_SP, S_SP + 2):
                c = (k - S_SP) // 2
                if layer == 0:
                    pe.wait_ge(dt_low_ready, 2 * s + 2)
                for t in range(2):
                    bank, done = fill(pe, B, f"dt{c}{t}")
                    if layer == 0:
                        mm = pe.matmul(bank[:, :], dt_w[:, c * P:(c + 1) * P], dt_low[:, t * HALF:(t + 1) * HALF],
                                       start=True, stop=True)
                    else:
                        for i in range(CH):
                            mm = pe.matmul(bank[:, :], delta_w[:, i, c * P:(c + 1) * P],
                                           xl[q][:, i, t * HALF:(t + 1) * HALF], start=(i == 0), stop=(i == CH - 1))
                    mm.then_inc(done, 1)

        value_done = sem("value_done")

        def value_read(eng, B, s, j):
            if j % 4 == 3:
                take(eng, B, f"values{j // 4}")
            else:
                eng.wait_ge(value_done, 3 * (TILES // 4) * s + 3 * (j // 4) + j % 4 + 1)

        def act_front(act, B, layer, s, g, q, k):
            if k == S_RSTD:
                act.wait_ge(ln_step, 3 * g + 2)
                act.activation(rstd[:, :], rstd[:, :], ACT.Ln).then_inc(rstd_ready, 1)
                act.wait_ge(rstd_ready, 2 * g + 1)
                act.activation(rstd[:, :], rstd[:, :], ACT.Exp, scale=-0.5).then_inc(rstd_ready, 1)
            if k == S_TURN:
                for n in range(2):
                    bank, done = take(act, B, f"tr{n}")
                    act.activation(xnT[:, n * HALF:(n + 1) * HALF], bank[:, :], ACT.Copy).then_inc(done, 1)
            for c in range(CH):
                if k == ((7, 8), (8, 10))[layer][c]:
                    if c == 0:
                        at_least(act, u_ready, g)
                    for t in range(2):
                        bank, done = take(act, B, f"x{c}{t}")
                        act.activation(conv_in[:, c, TAPS - 1 + t * HALF:TAPS - 1 + (t + 1) * HALF], bank[:, :],
                                       ACT.Copy).then_inc(done, 1)
            if layer == 0 and k == 7:
                bank, done = take(act, B, "logits")
                act.activation(probs[:, :, 0:E0], bank[:, 0:TILES * E0].rearrange("p (j e) -> p j e", e=E0),
                               ACT.Exp, scale=-1.0).then_inc(done, 1)
            if layer == 0:
                j = k - S_FFN - 1
                if 0 <= j < TILES:
                    bank, done = take(act, B, f"turn{j}")
                    if j >= 2:
                        value_read(act, B, s, j - 2)
                    act.activation(scoredT[j % 2], bank[:, :], ACT.Copy).then_inc(done, 1)
                j = k - S_FFN - 2
                if 0 <= j < TILES and j % 4 == 3:
                    j0 = j - 3
                    bank, done = take(act, B, f"values{j // 4}")
                    if j0 == 0:
                        at_least(act, back_step0, s - 1)
                    act.activation(g_tok[q][:, j0:j0 + 4, :], bank[:, :].rearrange("p (j d) -> p j d", d=DM),
                                   ACT.Copy).then_inc(done, 1)
            if k in (S_SP, S_SP + 2):
                c = (k - S_SP) // 2
                n = 4 * (CH * g + c)
                if layer == 1 and c == 0:
                    act.wait_ge(scattered, 16 * TILES * (s + 1))
                for t in range(2):
                    bank, done = take(act, B, f"dt{c}{t}")
                    act.activation(sp_z[c][:, t * HALF:(t + 1) * HALF], bank[:, :], ACT.Identity,
                                   bias=dt_b[layer][:, c:c + 1]).then_inc(done, 1)
                taken(act, B, f"dt{c}0")
                taken(act, B, f"dt{c}1")
                act.activation(sp_e[c], sp_z[c], ACT.Abs).then_inc(sp_act, 1)
                act.wait_ge(sp_act, n + 1)
                act.activation(sp_e[c], sp_e[c], ACT.Exp, scale=-1.0).then_inc(sp_act, 1)
            if k in (S_SP + 1, S_SP + 3):
                c = (k - S_SP - 1) // 2
                n = 4 * (CH * g + c)
                if c == 0 and layer_at(B[1] - 1) == 1:
                    act.wait_ge(back_step1, 5 * (B[0] - SEQS))
                act.wait_ge(sp_act, n + 2)
                act.activation(dt[q][:, c, :], sp_e[c], ACT.Copy, bias=1.0).then_inc(sp_act, 1)
                act.wait_ge(sp_act, n + 3)
                act.activation(sp_l[c], dt[q][:, c, :], ACT.Ln).then_inc(sp_act, 1)
                if layer == 0:
                    act.activation(sp_q[c], sp_e[c], ACT.Square, scale=0.5 ** 0.5).then_inc(square_ready, 1)
            if k == S_Z:
                act.wait_ge(conv_step, 8 * g + 1)
                for t in range(2):
                    bank, done = take(act, B, f"z0{t}")
                    act.activation(zs[q][:, 0, t * HALF:(t + 1) * HALF], bank[:, :], ACT.Copy).then_inc(done, 1)
            if k == S_SILU:
                act.wait_ge(conv_step, 8 * g + 8)
                for c in range(CH):
                    i = act.activation(xl[q][:, c, :], xl[q][:, c, :], ACT.Silu, bias=conv_b[layer][:, c:c + 1])
                i.then_inc(silu_ready, 1)
                for t in range(2):
                    bank, done = take(act, B, f"z1{t}")
                    act.activation(zs[q][:, 1, t * HALF:(t + 1) * HALF], bank[:, :], ACT.Silu).then_inc(done, 1)
                taken(act, B, "z00")
                taken(act, B, "z01")
                act.activation(zs[q][:, 0, :], zs[q][:, 0, :], ACT.Silu).then_inc(z_ready, 1)
                if layer == 0:
                    for n in range(2):
                        taken(act, B, f"values{n}")
                    act.activation(g_tok[q][:, :, :], g_tok[q][:, :, :], ACT.Silu).then_inc(g_ready, 1)
                nc.scalar.preload_act_table_set(EXP_LN)
            if k == S_PROJ:
                r = RANK if layer == 0 else 0
                for t in range(2):
                    cols = slice(t * HALF, (t + 1) * HALF)
                    bank, _ = take(act, B, f"proj{t}")
                    if layer == 0:
                        act.activation(dt_low[:, cols], bank[0:RANK, :], ACT.Copy).then_inc(dt_low_ready, 1)
                    if t == 0:
                        at_least(act, c_ready, UNITS * (g - 1))
                    act.activation(parts[q][0:2 * NS, cols], bank[r:r + 2 * NS, :], ACT.Copy).then_inc(hi_ready, 1)
            if k == S_PROJ + 2:
                for t in range(2):
                    cols = slice(t * HALF, (t + 1) * HALF)
                    taken(act, B, f"proj{t}")
                    act.activation(mid[q][:, cols], rest[q][:, cols], ACT.Copy).then_inc(mid_ready, 1)
                    act.wait_ge(mid_ready, 2 * g + t + 1)
                    act.activation(parts[q][2 * NS:4 * NS, cols], mid[q][:, cols], ACT.Copy).then_inc(mid_copied, 1)

        def dve_front(dve, B, layer, s, g, q, k):
            if k == S_STATS:
                dve.wait_ge(x_in, 16 * (g + 1))
                for j in range(TILES):
                    i = dve.bn_stats(stats[:, j, :], x_tok[:, j, :])
                i.then_inc(ln_step, 1)
                wait_apart(dve, ln_step, 3 * g + 1)
                for j in range(TILES):
                    i = dve.bn_aggr(mv[:, j, :], stats[:, j, :])
                i.then_inc(ln_extra, 1)
                dve.wait_ge(ln_extra, g + 1)
                dve.tensor_scalar(rstd[:, :], mv[:, :, 1], EPS, None, ALU.add).then_inc(ln_step, 1)
            if k == S_NORM:
                dve.wait_ge(rstd_ready, 2 * g + 2)
                for j in range(TILES):
                    i = dve.tensor_scalar(xn[:, j, :], x_tok[:, j, :], mv[:, j, 0:1], rstd[:, j:j + 1],
                                          ALU.subtract, ALU.mult)
                i.then_inc(ln_step, 1)
            if S_CONV[layer] <= k < S_CONV[layer] + 2 * TAPS:
                c, tap = divmod(k - S_CONV[layer], TAPS)
                src = conv_in[:, c, tap:tap + LEN]
                w = conv_w[layer][:, c, tap:tap + 1]
                if tap == 0:
                    taken(dve, B, f"x{c}0")
                    taken(dve, B, f"x{c}1")
                    if layer_at(B[1] - 1) == 1:
                        for n in range(2):
                            j, cnt = use(B, f"out{n}")
                            dve.wait_ge(full[j], cnt)
                    dve.tensor_scalar(xl[q][:, c, :], src, w, None, ALU.mult).then_inc(conv_step, 1)
                else:
                    dve.wait_ge(conv_step, 8 * g + TAPS * c + tap)
                    dve.scalar_tensor_tensor(xl[q][:, c, :], src, w, xl[q][:, c, :], ALU.mult,
                                             ALU.add).then_inc(conv_step, 1)
            if layer == 0 and k == S_GATE[0]:
                n = 9 * s
                taken(dve, B, "logits")
                dve.tensor_scalar(replaced[:, :, 0:E0], probs[:, :, 0:E0], 1.0, None, ALU.add).then_inc(gate_step0, 1)
                dve.wait_ge(gate_step0, n + 1)
                dve.reciprocal(probs[:, :, 0:E0], replaced[:, :, 0:E0]).then_inc(gate_step0, 1)
                wait_apart(dve, gate_step0, n + 2)
                for j in range(TILES):
                    i = dve.max(top[:, j, :], probs[:, j, 0:E0])
                i.then_inc(gate_step0, 1)
                dve.wait_ge(gate_step0, n + 3)
                dve.tensor_copy(wanted[:, :, 0:K0], top[:, :, 0:K0]).then_inc(gate_step0, 1)
            if layer == 0 and k == S_GATE[0] + 1:
                n = 9 * s
                wait_apart(dve, gate_step0, n + 4)
                for j in range(TILES):
                    i = dve.match_replace(replaced[:, j, 0:E0 + 8 - K0], wanted[:, j, 0:8],
                                          probs[:, j, 0:E0 + 8 - K0], -1.0)
                i.then_inc(gate_step0, 1)
                dve.wait_ge(gate_step0, n + 5)
                dve.scalar_tensor_tensor(share[:, :, :], replaced[:, :, 0:E0], 0.0, probs[:, :, 0:E0], ALU.is_lt,
                                         ALU.mult).then_inc(gate_step0, 1)
                dve.wait_ge(gate_step0, n + 6)
                dve.tensor_reduce(share_sum[:, :], share[:, :, :], AX.X, ALU.add).then_inc(gate_step0, 1)
                dve.wait_ge(gate_step0, n + 7)
                dve.tensor_scalar(share_sum[:, :], share_sum[:, :], 1e-9, None, ALU.max).then_inc(gate_extra, 1)
                dve.wait_ge(gate_extra, 2 * s + 1)
                dve.reciprocal(share_sum[:, :], share_sum[:, :]).then_inc(gate_step0, 1)
                dve.wait_ge(gate_step0, n + 8)
                dve.tensor_scalar(share_sum[:, :], share_sum[:, :], route[:, 0:1], None, ALU.mult).then_inc(gate_extra, 1)
                dve.wait_ge(gate_extra, 2 * s + 2)
                dve.tensor_tensor(share[:, :, :], share[:, :, :],
                                  share_sum[:, :].unsqueeze(2).to_broadcast([P, TILES, E0]), ALU.mult).then_inc(gate_step0, 1)
            if layer == 0 and S_FFN <= k < S_FFN + TILES:
                j = k - S_FFN
                if j == 0:
                    dve.wait_ge(gate_step0, 9 * s + 9)
                bank, done = take(dve, B, f"score{j}")
                if j >= 2:
                    jt, cnt = use(B, f"turn{j - 2}")
                    dve.wait_ge(full[jt], cnt)
                dve.scalar_tensor_tensor(scored[j % 2].rearrange("p (e h) -> p e h", h=EH),
                                         bank[:, :].rearrange("p (e h) -> p e h", h=EH), 0.0,
                                         share[:, j, :].unsqueeze(2).to_broadcast([P, E0, EH]),
                                         ALU.max, ALU.mult).then_inc(done, 1)
            if layer == 1 and k == S_GATE[1]:
                n = 5 * s
                bank, done = take(dve, B, "logits")
                logits = probs[:, :, E1:2 * E1]
                dve.tensor_tensor(logits, bank[:, 0:TILES * E1].rearrange("p (j e) -> p j e", e=E1),
                                  gate_b[:, :].unsqueeze(1).to_broadcast([P, TILES, E1]), ALU.add).then_inc(done, 1)
                taken(dve, B, "logits")
                dve.tensor_tensor(logits, logits,
                                  expert_bias[:, :].unsqueeze(1).to_broadcast([P, TILES, E1]), ALU.add).then_inc(gate_step1, 1)
                wait_apart(dve, gate_step1, n + 1)
                for j in range(TILES):
                    i = dve.max(top[:, j, :], probs[:, j, E1:2 * E1])
                i.then_inc(gate_step1, 1)
                dve.wait_ge(gate_step1, n + 2)
                dve.tensor_copy(wanted[:, :, 8:9], top[:, :, 0:1]).then_inc(gate_step1, 1)
            if layer == 1 and k == S_GATE[1] + 1:
                n = 5 * s
                wait_apart(dve, gate_step1, n + 3)
                for j in range(TILES):
                    i = dve.match_replace(replaced[:, j, 0:2 * E1 - 1], wanted[:, j, 8:16], probs[:, j, E1:3 * E1 - 1],
                                          -SENTINEL)
                i.then_inc(gate_step1, 1)
                dve.wait_ge(gate_step1, n + 4)
                dve.tensor_scalar(onehot[:, :, :], replaced[:, :, 0:E1], -SENTINEL, None, ALU.is_le).then_inc(gate_step1, 1)
            for c in range(CH):
                n = 3 * (CH * g + c)
                d = dt[q][:, c, :]
                if k == S_SP + 2 + 2 * c:
                    dve.wait_ge(sp_act, 4 * (CH * g + c) + 4)
                    dve.scalar_tensor_tensor(d, d, -1.0, sp_e[c], ALU.add, ALU.subtract).then_inc(sp_dve, 1)
                    dve.wait_ge(sp_dve, n + 1)
                    dve.tensor_tensor(d, sp_l[c], d, ALU.subtract).then_inc(sp_dve, 1)
                if k == S_SP + 3 + 2 * c:
                    if layer == 0:
                        dve.wait_ge(square_ready, CH * s + c + 1)
                        dve.tensor_tensor(sp_q[c], sp_e[c], sp_q[c], ALU.subtract).then_inc(series_ready, 1)
                        dve.wait_ge(series_ready, 2 * (CH * s + c) + 1)
                        dve.wait_ge(sp_dve, n + 2)
                        dve.scalar_tensor_tensor(d, d, -LN_ERROR, sp_q[c], ALU.add, ALU.max).then_inc(series_ready, 1)
                        dve.wait_ge(series_ready, 2 * (CH * s + c) + 2)
                    else:
                        dve.wait_ge(sp_dve, n + 2)
                    dve.scalar_tensor_tensor(d, sp_z[c], 0.0, d, ALU.max, ALU.add).then_inc(sp_dve, 1)
                    if layer == 1:
                        dve.wait_ge(sp_dve, n + 3)
                        dve.tensor_scalar(d, d, 1e-4, 10.0, ALU.max, ALU.min).then_inc(clipped, 1)
            if layer == 1 and k == 13:
                n = 4 * s
                bank, _ = take(dve, B, "ranks")
                dve.tensor_tensor(marks[:, 0:E1, :], bank[:, TILES * E1:(TILES + 1) * E1].unsqueeze(2)
                                  .to_broadcast([P, E1, E1]), tile_sizes[:, :, :], ALU.is_gt).then_inc(slot_step, 1)
                dve.wait_ge(slot_step, n + 1)
                dve.tensor_reduce(blocks_of[:, :], marks[:, 0:E1, :], AX.X, ALU.add).then_inc(slot_step, 1)
                dve.wait_ge(slot_step, n + 2)
                dve.tensor_tensor_scan(block_end[:, :], ones_e[:, :], blocks_of[:, :], 0.0, ALU.mult,
                                       ALU.add).then_inc(slot_step, 1)
                dve.wait_ge(slot_step, n + 3)
                dve.tensor_tensor(first_slot[:, :], block_end[:, :], blocks_of[:, :], ALU.subtract).then_inc(slot_step, 1)
            if layer == 1 and k == 14:
                n = 4 * s
                bank, done = take(dve, B, "ranks")
                dve.wait_ge(slot_step, n + 4)
                dve.scalar_tensor_tensor(place[:, :, :], first_slot[:, :].unsqueeze(1).to_broadcast([P, TILES, E1]), float(P),
                                         bank[:, 0:TILES * E1].rearrange("p (j e) -> p j e", e=E1), ALU.mult,
                                         ALU.add).then_inc(done, 1)
                taken(dve, B, "ranks")
                dve.tensor_tensor(place[:, :, :], place[:, :, :], onehot[:, :, :], ALU.mult).then_inc(place_step, 1)
                dve.wait_ge(place_step, 2 * s + 1)
                dve.tensor_reduce(place_sum[:, :], place[:, :, :], AX.X, ALU.add).then_inc(place_step, 1)
                dve.wait_ge(place_step, 2 * s + 2)
                at_least(dve, gathered, 16 * TILES * (s - 1))
                dve.tensor_copy(slot_of[q][:, :], place_sum[:, :]).then_inc(slots_ready, 1)
            if layer == 1 and k == 15:
                n = 3 * s
                dve.tensor_tensor(marks[:, :, :], block_end[:, :].unsqueeze(1).to_broadcast([P, BLOCKS, E1]),
                                  tile_numbers[:, :, :], ALU.is_le).then_inc(expert_step, 1)
                dve.wait_ge(expert_step, 2 * s + 1)
                dve.tensor_reduce(expert_f[:, :], marks[:, :, :], AX.X, ALU.add).then_inc(expert_step, 1)
                dve.wait_ge(expert_step, 2 * s + 2)
                for j in range(2):
                    at_least(dve, expert_in[j], 16 * PER_BODY[j] * (s - 1))
                dve.tensor_scalar(block_expert[q][:, :], expert_f[:, :], float(E1 - 1), None, ALU.min)\
                    .then_inc(experts_ready, 1)
            if k == S_PROJ + 1:
                r = RANK if layer == 0 else 0
                for t in range(2):
                    cols = slice(t * HALF, (t + 1) * HALF)
                    bank, done = take(dve, B, f"proj{t}")
                    dve.wait_ge(hi_ready, 2 * g + t + 1)
                    dve.tensor_tensor(rest[q][:, cols], bank[r:r + 2 * NS, :], parts[q][0:2 * NS, cols],
                                      ALU.subtract).then_inc(done, 1)
            if k == S_PROJ + 3:
                for t in range(2):
                    cols = slice(t * HALF, (t + 1) * HALF)
                    taken(dve, B, f"proj{t}")
                    dve.wait_ge(mid_ready, 2 * g + t + 1)
                    dve.tensor_tensor(parts[q][4 * NS:6 * NS, cols], rest[q][:, cols], mid[q][:, cols],
                                      ALU.subtract).then_inc(lo_ready, 1)
            if k == S_U:
                dve.wait_ge(sp_dve, 3 * CH * (g + 1))
                if layer == 1:
                    dve.wait_ge(clipped, CH * (s + 1))
                dve.wait_ge(silu_ready, g + 1)
                dve.wait_ge(mid_copied, 2 * g + 2)
                dve.wait_ge(lo_ready, 2 * g + 2)
                dve.tensor_tensor(u[q][:, :, :], dt[q][:, :, :], xl[q][:, :, :], ALU.mult).then_inc(u_ready, 1)

        ln_extra = sem("ln_extra")
        gate_extra = sem("gate_extra")
        clipped = sem("clipped")
        square_ready, series_ready = sem("square_ready"), sem("series_ready")

        def unit(g, k, lag):
            return (g, k - lag) if k >= lag else (g - 1, k - lag + UNITS)

        def none(g, k):
            return isinstance(g, int) and (g < 0 or g >= 2 * SEQS)

        def count(g, k):
            return g * UNITS + (k + 1)

        def pe_core(pe, g, k, p):
            if not none(g, k):
                tc, n = divmod(k, NS)
                cols = slice(tc * HALF, (tc + 1) * HALF)
                if k == 0:
                    pe.wait_ge(hi_ready, 2 * g + 2)
                    pe.wait_ge(mid_copied, 2 * g + 2)
                    pe.wait_ge(lo_ready, 2 * g + 2)
                at_least(pe, inject_ready, count(g, k) - 2)
                pe.matmul(b_ps[k % 2][:, :], spread[:, n, :], parts[p][:, cols], start=True, stop=True).then_inc(b_ready, 1)
                at_least(pe, c_copied, count(g, k) - 1)
                pe.matmul(c_ps[:, :], spread[:, NS + n, :], parts[p][:, cols], start=True, stop=True).then_inc(c_ready, 1)
            gr, kr = unit(g, k, R_LAG)
            if not none(gr, kr):
                tc, n = divmod(kr, NS)
                pe.wait_ge(weighted_ready, count(gr, kr))
                if n == 0:
                    at_least(pe, y_taken, gr * 2 + tc)
                for c in range(CH):
                    mm = pe.matmul(y_ps[c][:, :], ident[:, :], weighted[kr % 4][:, c, :], start=(n == 0), stop=(n == NS - 1))
                mm.then_inc(summed, 1)

        def act_core(act, g, k, p, layer):
            if none(g, k):
                return
            tc, n = divmod(k, NS)
            cols = slice(tc * HALF, (tc + 1) * HALF)
            act.wait_ge(c_ready, count(g, k))
            at_least(act, weighted_ready, count(g, k) - 2)
            act.activation(c_sb[k % 2][:, :], c_ps[:, :], ACT.Copy).then_inc(c_copied, 1)
            at_least(act, scanned, count(g, k) - 2)
            if k == 0:
                act.wait_ge(u_ready, g + 1)
            for c in range(CH):
                i = act.activation(decay[k % 2][:, c, :], dt[p][:, c, cols], ACT.Exp, scale=A[layer][:, c, n:n + 1])
            i.then_inc(decay_ready, 1)

        def dve_core(dve, g, k, p):
            if not none(g, k):
                tc, n = divmod(k, NS)
                cols = slice(tc * HALF, (tc + 1) * HALF)
                if k == 0:
                    dve.wait_ge(u_ready, g + 1)
                dve.wait_ge(b_ready, count(g, k))
                at_least(dve, scanned, count(g, k) - 2)
                dve.tensor_tensor(inject[k % 2][:, :, :], u[p][:, :, cols],
                                  b_ps[k % 2][:, :].unsqueeze(1).to_broadcast([P, CH, HALF]), ALU.mult).then_inc(inject_ready, 1)
            gs, ks = unit(g, k, 1)
            if not none(gs, ks):
                tc, n = divmod(ks, NS)
                dve.wait_ge(inject_ready, count(gs, ks))
                dve.wait_ge(decay_ready, count(gs, ks))
                at_least(dve, weighted_ready, count(gs, ks) - 2)
                if ks < NS + 2:
                    at_least(dve, carried, gs * NS + ks - 1)
                for c in range(CH):
                    i = dve.tensor_tensor_scan(hs[ks % 2][:, c, :], decay[ks % 2][:, c, :], inject[ks % 2][:, c, :],
                                               carry[:, n, c:c + 1] if tc else 0.0, ALU.mult, ALU.add)
                i.then_inc(scanned, 1)

        def pool_core(pool, g, k):
            if none(g, k):
                return
            tc, n = divmod(k, NS)
            pool.wait_ge(scanned, count(g, k))
            pool.wait_ge(c_copied, count(g, k))
            at_least(pool, summed, count(g, k) - 4)
            pool.tensor_tensor(weighted[k % 4][:, :, :], hs[k % 2][:, :, :],
                               c_sb[k % 2][:, :].unsqueeze(1).to_broadcast([P, CH, HALF]), ALU.mult).then_inc(weighted_ready, 1)
            if tc == 0:
                pool.tensor_copy(carry[:, n, :], hs[k % 2][:, :, HALF - 1]).then_inc(carried, 1)

        def dve_take_y(dve, g, tc, p, layer):
            cols = slice(tc * HALF, (tc + 1) * HALF)
            dve.wait_ge(summed, count(g, tc * NS + NS - 1))
            at_least(dve, z_ready, g + 1)
            if layer == 0:
                for c in range(CH):
                    i = dve.scalar_tensor_tensor(xl[p][:, c, cols], xl[p][:, c, cols], skip_d[:, c:c + 1],
                                                 y_ps[c][:, :], ALU.mult, ALU.add)
                i.then_inc(y_taken, 1)
                dve.wait_ge(y_taken, 2 * g + tc + 1)
                dve.tensor_tensor(xl[p][:, :, cols], xl[p][:, :, cols], zs[p][:, :, cols], ALU.mult).then_inc(evac, 1)
            else:
                for c in range(CH):
                    i = dve.tensor_tensor(xl[p][:, c, cols], zs[p][:, c, cols], y_ps[c][:, :], ALU.mult)
                i.then_inc(y_taken, 1)

        def pe_back(pe, B, layer, s, g, p, k):
            if k == (5, 11)[layer]:
                if layer == 0:
                    pe.wait_ge(evac, 2 * g + 2)
                for n in range(2):
                    bank, done = fill(pe, B, f"out{n}")
                    for j in range(4):
                        cols = slice((4 * n + j) * P, (4 * n + j + 1) * P)
                        for c in range(CH):
                            mm = pe.matmul(bank[:, j * DM:(j + 1) * DM], xl[p][:, c, cols], out_w[layer][:, c, :],
                                           start=(c == 0), stop=(c == CH - 1))
                    mm.then_inc(done, 1)
            if layer == 1 and k in (5, 7):
                if k == 5:
                    pe.wait_ge(y_taken, 2 * g + 2)
                for n in (0, 1) if k == 5 else (2, 3):
                    bank, done = fill(pe, B, f"turned{n}")
                    for j in range(2):
                        for c in range(CH):
                            mm = pe.transpose(bank[:, (2 * j + c) * P:(2 * j + c + 1) * P],
                                              xl[p][:, c, (2 * n + j) * P:(2 * n + j + 1) * P], ident[:, :])
                    mm.then_inc(done, 1)

        def dve_back(dve, B, layer, s, g, p, k):
            if layer == 0 and k == 6:
                dve.wait_ge(g_ready, g + 1)
                for n in range(2):
                    tiles = slice(4 * n, 4 * n + 4)
                    bank, done = take(dve, B, f"out{n}")
                    dve.tensor_tensor(sum_tok[:, tiles, :], bank[:, :].rearrange("p (j d) -> p j d", d=DM),
                                      g_tok[p][:, tiles, :], ALU.mult).then_inc(done, 1)
            if layer == 0 and k == 7:
                taken(dve, B, "out0")
                taken(dve, B, "out1")
                dve.wait_ge(x_back_in, 16 * (g + 1))
                dve.tensor_tensor(x_back[:, :, :], x_back[:, :, :], sum_tok[:, :, :], ALU.add).then_inc(back_step0, 1)
            if layer == 1 and k in (6, 8):
                for n in (0, 1) if k == 6 else (2, 3):
                    bank, done = take(dve, B, f"turned{n}")
                    for j in range(2):
                        i = dve.bn_stats(out_stats[:, 2 * n + j, :], bank[:, 2 * j * P:2 * (j + 1) * P])
                    i.then_inc(done, 1)
            if layer == 1 and k == 8:
                for n in range(4):
                    taken(dve, B, f"turned{n}")
                dve.tensor_copy(idle[:, 1:2], idle[:, 0:1])
                for j in range(TILES):
                    i = dve.bn_aggr(out_mv[:, j, :], out_stats[:, j, :])
                i.then_inc(back_step1, 1)
                dve.wait_ge(back_step1, 5 * s + 1)
                dve.tensor_scalar(out_r[:, :], out_mv[:, :, 1], EPS, None, ALU.add).then_inc(back_step1, 1)
            if layer == 1 and k == 10:
                dve.wait_ge(back_act, 2 * s + 2)
                dve.scalar_tensor_tensor(out_nm[:, :], out_mv[:, :, 0], -1.0, out_r[:, :], ALU.mult, ALU.mult)\
                    .then_inc(back_step1, 1)
                dve.wait_ge(back_step1, 5 * s + 3)
                for j in range(TILES):
                    i = dve.scalar_tensor_tensor(sum_tok[:, j, :], gain_sum[:, :], out_nm[:, j:j + 1], bias_out[:, :],
                                                 ALU.mult, ALU.add)
                i.then_inc(back_sum, 1)
            for n in range(2 if layer == 1 and k == 12 else 0):
                if n == 0:
                    dve.wait_ge(back_sum, s + 1)
                bank, done = take(dve, B, f"out{n}")
                for j in range(4):
                    m = 4 * n + j
                    i = dve.scalar_tensor_tensor(sum_tok[:, m, :], bank[:, j * DM:(j + 1) * DM],
                                                 out_r[:, m:m + 1], sum_tok[:, m, :], ALU.mult, ALU.add)
                i.then_inc(done, 1)
            if layer == 1 and k == 23:
                taken(dve, B, "out0")
                taken(dve, B, "out1")
                dve.wait_ge(g_ready, g + 1)
                dve.tensor_tensor(sum_tok[:, :, :], sum_tok[:, :, :], g_tok[p][:, :, :], ALU.mult).then_inc(back_step1, 1)
                dve.wait_ge(back_step1, 5 * s + 4)
                dve.wait_ge(x_back_in, 16 * (g + 1))
                dve.tensor_tensor(x_back[:, :, :], x_back[:, :, :], sum_tok[:, :, :], ALU.add).then_inc(back_step1, 1)

        def act_back(act, B, layer, s, g, p, k):
            if layer == 1 and k == S_SILU:
                act.wait_ge(gathered, 16 * TILES * (s + 1))
                act.activation(g_tok[p][:, :, :], g_tok[p][:, :, :], ACT.Silu).then_inc(g_ready, 1)
                if B[1] == 2 * SEQS - 1:
                    nc.scalar.preload_act_table_set(EXP_LN)
            if layer == 1 and k == 9:
                act.wait_ge(back_step1, 5 * s + 2)
                act.activation(out_r[:, :], out_r[:, :], ACT.Ln).then_inc(back_act, 1)
                act.wait_ge(back_act, 2 * s + 1)
                act.activation(out_r[:, :], out_r[:, :], ACT.Exp, scale=-0.5).then_inc(back_act, 1)

        def layer_of(g, static):
            return 0 if static < SEQS else 1

        def over_bodies(eng, body):
            body(-1, -1)
            body(0, 0)
            for layer in range(2):
                first = SEQS * layer + 1
                with eng.Fori(0, (SEQS - 2) // 2) as i:
                    for m in range(2):
                        body(first + m + 2 * i, first + m)
                body(SEQS * layer + SEQS - 1, SEQS * layer + SEQS - 1)
                if layer == 0:
                    body(SEQS, SEQS)
            body(2 * SEQS, 2 * SEQS)

        def local(g, like):
            return (0, g) if like < SEQS else (1, g - SEQS)

        @block.sync
        def _(sp):
            for dst, name in plain:
                sp.dma_start(dst[:], T[name]).then_inc(loaded, 16)
            sp.dma_start(side_w[:, :], T["side_w"]).then_inc(loaded, 16)
            for dst, name, n in ((tile_sizes, "tile_sizes", E1 * E1), (tile_numbers, "tile_numbers", BLOCKS * E1)):
                sp.dma_start(dst[:, :, :].rearrange("p a b -> p (a b)"),
                             T[name].rearrange("(a n) -> a n", a=1).to_broadcast([P, n])).then_inc(loaded, 16)
            sp.wait_ge(prep, PREP_ZERO)
            for j in range(2):
                for i in range(BLOCKS):
                    sp.dma_start(T[f"sorted_x{j}"][i * P:(i + 1) * P, :], zeros[:, :])\
                        .then_inc(zeroed if i else stored, 16)
            for dst, name, n in spreads:
                sp.dma_start(dst[:, :], T[name].rearrange("(a n) -> a n", a=1).to_broadcast([P, n])).then_inc(loaded, 16)
            sp.dma_start(A[1][:, 0, :], T["A_log1"].rearrange("(a n) -> a n", a=1).to_broadcast([P, NS])).then_inc(loaded, 16)

            def body(g, like):
                for k in range(UNITS):
                    if like >= 1:
                        layer, s = local(g - 1, like - 1)
                        sp_back(sp, layer, s, g - 1, k)
                    if like + 1 < 2 * SEQS:
                        layer, s = local(g + 1, like + 1)
                        sp_front(sp, (g, like), layer, s, g + 1, (like + 1) % 2, k)
                    if layer_at(like) == 1:
                        sp_blocks(sp, (g, like), g - SEQS, like % 2, k)

            over_bodies(sp, body)
            sp.wait_ge(stored, 16 * (2 * SEQS + 2))

        @block.tensor
        def _(pe):
            pe.wait_ge(loaded, N_LOADS)
            pe.wait_ge(prep, PREP_ONES)
            for c in range(CH):
                mm = pe.matmul(side_ps[2][:, 0:DM], one_col[:, c, :], out_w[1][:, c, :], start=(c == 0), stop=(c == CH - 1))
            mm.then_inc(prep_pe, 1)
            pe.wait_ge(prep, PREP_GAIN)
            for c in range(CH):
                mm = pe.matmul(side_ps[2][:, DM:2 * DM], one_col[:, c, :], out_w[1][:, c, :], start=(c == 0), stop=(c == CH - 1))
            mm.then_inc(prep_pe, 1)
            pe.wait_ge(prep, PREP_ALL)

            def body(g, like):
                for k in range(UNITS):
                    pe_core(pe, g, k, like % 2)
                    if like == 2 * SEQS and k > LAST_BACK:
                        return
                    if like >= 1:
                        layer, s = local(g - 1, like - 1)
                        pe_back(pe, (g, like), layer, s, g - 1, (like - 1) % 2, k)
                    if like + 1 < 2 * SEQS:
                        layer, s = local(g + 1, like + 1)
                        pe_front(pe, (g, like), layer, s, g + 1, (like + 1) % 2, k)
                    if layer_at(like) == 1:
                        pe_blocks(pe, (g, like), g - SEQS, k)

            over_bodies(pe, body)

        @block.scalar
        def _(act):
            nc.scalar.preload_act_table_set(EXP_LN)
            act.wait_ge(loaded, N_LOADS)
            act.activation(A[0][:, :, :], A[0][:, :, :], ACT.Exp).then_inc(prep_act, 1)
            act.activation(small[:, 0, 0:NS], A[1][:, 0, :], ACT.Abs).then_inc(prep_act, 1)
            act.wait_ge(prep_act, 2)
            act.activation(small[:, 1, 0:NS], small[:, 0, 0:NS], ACT.Exp, scale=-1.0).then_inc(prep_act, 1)
            act.wait_ge(prep_act, 3)
            act.activation(small[:, 3, 0:NS], small[:, 1, 0:NS], ACT.Copy, bias=1.0).then_inc(prep_act, 1)
            act.wait_ge(prep_act, 4)
            act.activation(small[:, 2, 0:NS], small[:, 3, 0:NS], ACT.Ln).then_inc(prep_act, 1)
            act.wait_ge(prep, PREP_ALL)

            def body(g, like):
                for k in range(UNITS):
                    if like >= 0 and like < 2 * SEQS:
                        act_core(act, g, k, like % 2, int(like >= SEQS))
                    if like >= 1:
                        layer, s = local(g - 1, like - 1)
                        act_back(act, (g, like), layer, s, g - 1, (like - 1) % 2, k)
                    if like + 1 < 2 * SEQS:
                        layer, s = local(g + 1, like + 1)
                        act_front(act, (g, like), layer, s, g + 1, (like + 1) % 2, k)
                    if layer_at(like) == 1:
                        act_blocks(act, (g, like), g - SEQS, k)

            over_bodies(act, body)

        @block.vector
        def _(dve):
            step = [0]

            def link(i):
                step[0] += 1
                i.then_inc(prep, 1)
                dve.wait_ge(prep, step[0])

            link(dve.memset(zeros[:, :], 0.0))
            dve.wait_ge(loaded, N_LOADS)
            link(dve.memset(one_col[:, :, :], 0.0))
            for c in range(CH):
                link(dve.tensor_scalar(one_col[:, c, :], one_col[:, c, :], ln_b[:, c:c + 1], None, ALU.add))
            assert step[0] == PREP_ONES
            dve.wait_ge(prep_pe, 1)
            for c in range(CH):
                link(dve.tensor_scalar(out_w[1][:, c, :], out_w[1][:, c, :], ln_g[:, c:c + 1], None, ALU.mult))
            link(dve.memset(one_col[:, :, :], 1.0))
            assert step[0] == PREP_GAIN
            dve.wait_ge(prep_pe, 2)
            link(dve.tensor_copy(bias_out[:, :], side_ps[2][:, 0:DM]))
            link(dve.tensor_copy(gain_sum[:, :], side_ps[2][:, DM:2 * DM]))
            link(dve.memset(ones_e[:, :], 1.0))
            link(dve.memset(idle[:, :], 0.0))
            link(dve.memset(probs[:, :, :], SENTINEL))
            link(dve.memset(wanted[:, :, :], SENTINEL))
            link(dve.memset(conv_in[:, :, 0:TAPS - 1], 0.0))
            link(dve.tensor_copy(spread[:, :, :], part_rows[:, :].unsqueeze(2).to_broadcast([96, 2 * NS, P])))
            dve.wait_ge(prep_act, 5)
            link(dve.tensor_scalar(A[0][:, :, :], A[0][:, :, :], -1.0, None, ALU.mult))
            link(dve.scalar_tensor_tensor(small[:, 3, 0:NS], small[:, 3, 0:NS], -1.0, small[:, 1, 0:NS], ALU.add,
                                          ALU.subtract))
            link(dve.tensor_tensor(small[:, 3, 0:NS], small[:, 2, 0:NS], small[:, 3, 0:NS], ALU.subtract))
            link(dve.scalar_tensor_tensor(small[:, 3, 0:NS], A[1][:, 0, :], 0.0, small[:, 3, 0:NS], ALU.max, ALU.add))
            for c in range(CH):
                link(dve.tensor_scalar(A[1][:, c, :], small[:, 3, 0:NS], -1.0, None, ALU.mult))
            assert step[0] == PREP_ALL, step[0]

            def body(g, like):
                for k in range(UNITS):
                    dve_core(dve, g, k, like % 2)
                    if like >= 1 and k == R_LAG:
                        dve_take_y(dve, g - 1, 1, (like - 1) % 2, int(like - 1 >= SEQS))
                    if 0 <= like < 2 * SEQS and k == NS + R_LAG - 1:
                        dve_take_y(dve, g, 0, like % 2, int(like >= SEQS))
                    if like >= 1:
                        layer, s = local(g - 1, like - 1)
                        dve_back(dve, (g, like), layer, s, g - 1, (like - 1) % 2, k)
                    if like == 2 * SEQS and k > LAST_BACK:
                        return
                    if like + 1 < 2 * SEQS:
                        layer, s = local(g + 1, like + 1)
                        dve_front(dve, (g, like), layer, s, g + 1, (like + 1) % 2, k)
                    if layer_at(like) == 1:
                        dve_blocks(dve, (g, like), g - SEQS, k)

            over_bodies(dve, body)

        @block.gpsimd
        def _(pool):
            def body(g, like):
                for k in range(UNITS):
                    front = g + 1 - SEQS if layer_at(like + 1) == 1 else None
                    back = g - 1 - SEQS if layer_at(like - 1) == 1 else None
                    pool_waits(pool, front, back, k)
                    if 0 <= like < 2 * SEQS:
                        pool_core(pool, g, k)
                    pool_indirect(pool, front, back, (like + 1) % 2, k)

            over_bodies(pool, body)


PREP_ZERO = 1
PREP_ONES = PREP_ZERO + 1 + CH
PREP_GAIN = PREP_ONES + CH + 1
PREP_ALL = PREP_GAIN + 8 + 4 + CH


def kernel(**inputs):
    import ml_dtypes
    import numpy as np
    import concourse.bacc as bacc
    from concourse.bass_utils import run_bass_kernel_spmd

    w = {k: np.asarray(v) for k, v in inputs.items()}

    def halves(a):
        return a.reshape((CH, P) + a.shape[1:]).swapaxes(0, 1)

    data = {
        "x": w["L0_attn_hidden_states"].reshape(SEQS * LEN, DM),
        "ident": np.eye(P, dtype=np.float32),
        "part_rows": np.tile(np.eye(2 * NS, dtype=np.float32), (3, 1)),
        "in_w": w["L0_attn_in_proj_w"].T,
        "conv_w0": halves(w["L0_attn_conv_w"]),
        "conv_b0": halves(w["L0_attn_conv_b"]),
        "x_w": halves(w["L0_attn_x_proj_w"].T),
        "dt_w": w["L0_attn_dt_proj_w"].T,
        "dt_b0": halves(w["L0_attn_dt_proj_b"]),
        "A_log0": halves(w["L0_attn_A_log"]),
        "skip_d": halves(w["L0_attn_D"]),
        "out_w0": halves(w["L0_attn_out_proj_w"].T),
        "sel_w": w["L0_ffn_expert_sel"].T,
        "keys": w["L0_ffn_keys"].transpose(1, 0, 2).reshape(DM, E0 * EH),
        "values": w["L0_ffn_values"].reshape(4, P, DM).transpose(1, 0, 2),
        "route": w["L0_ffn_route_scale"],
        "side_w": np.concatenate([w["L1_attn_W_left"].T, w["L1_attn_W_right"].T], axis=1),
        "conv_w1": halves(w["L1_attn_conv_w"][:, 0, :]),
        "conv_b1": halves(w["L1_attn_conv_b"]),
        "delta_w": halves(w["L1_attn_W_delta"].T),
        "dt_b1": halves(w["L1_attn_b_delta"]),
        "bc_w": halves(np.concatenate([w["L1_attn_W_B"], w["L1_attn_W_C"]], axis=0).T),
        "A_log1": w["L1_attn_A_log"],
        "ln_g": halves(w["L1_attn_ln_g"]),
        "ln_b": halves(w["L1_attn_ln_b"]),
        "out_w1": halves(w["L1_attn_W_out"].T),
        "gate_w": w["L1_ffn_gate_w"].T,
        "gate_b": w["L1_ffn_gate_b"],
        "expert_bias": w["L1_ffn_expert_bias"],
        "experts": np.concatenate([
            w["L1_ffn_w1"],
            w["L1_ffn_w2"].reshape(E1, FB, P, DM).transpose(0, 2, 1, 3).reshape(E1, P, FF),
            w["L1_ffn_b1"].reshape(E1, FB, P).transpose(0, 2, 1),
            np.broadcast_to(w["L1_ffn_b2"][:, None, :], (E1, P, DM))], axis=2),
        "before": np.triu(np.ones((P, P), np.float32), 1).astype(ml_dtypes.bfloat16),
        "ones": np.ones((P, P), ml_dtypes.bfloat16),
        "tile_sizes": np.tile(np.arange(E1, dtype=np.float32) * P, E1),
        "tile_numbers": np.repeat(np.arange(BLOCKS, dtype=np.float32), E1),
    }
    nc = bacc.Bacc("TRN2", target_bir_lowering=False, num_devices=1)
    arrays, T = {}, {}
    for name, a in data.items():
        arrays[f"in_{name}"] = np.ascontiguousarray(a)
        T[name] = nc.dram_tensor(f"in_{name}", a.shape, mybir.dt.from_np(a.dtype), kind="ExternalInput").ap()
    T["x1"] = nc.dram_tensor("x1", (SEQS * LEN, DM), F32, kind="Internal").ap()
    for j in range(2):
        T[f"sorted_x{j}"] = nc.dram_tensor(f"sorted_x{j}", (BLOCKS * P, DM), F32, kind="Internal").ap()
        T[f"sorted_y{j}"] = nc.dram_tensor(f"sorted_y{j}", (BLOCKS * P, DM), F32, kind="Internal").ap()
    out = nc.dram_tensor("out_x", (SEQS * LEN, DM), F32, kind="ExternalOutput").ap()
    build(nc, T, out)
    r = run_bass_kernel_spmd(nc, [arrays], core_ids=[0])
    return r.results[0]["out_x"].reshape(SEQS, LEN, DM)
```

```python
from contextlib import ExitStack

import concourse.bass as bass
from concourse import mybir

ALU = mybir.AluOpType
ACT = mybir.ActivationFunctionType
AX = mybir.AxisListType
F32 = mybir.dt.float32
I32 = mybir.dt.int32
BF16 = mybir.dt.bfloat16
EXP_LN = "natural_log_exp_and_others"

P = 128
SEQS, LEN, DM = 8, 1024, 128
CH = 2
HALF = LEN // 2
TILES = LEN // P
NS = 16
UNITS = 2 * NS
TAPS = 4
RANK = 64
E0, K0, EH = 16, 4, 32
E1, FF = 8, 512
FB = FF // P
BLOCKS = LEN // P + E1 - 1
R_LAG = 3
SENTINEL = 3.0e38
EPS = 1e-5
LN_ERROR = 4e-9


def at_least(eng, sem, value):
    if isinstance(value, int) and value <= 0:
        return
    eng.wait_ge(sem, value)


def build(nc, T, out):
    ctx = ExitStack()
    with ctx:
        def sb(name, shape, dt=F32):
            return ctx.enter_context(nc.sbuf_tensor(name, shape, dt))

        def pb(name):
            return ctx.enter_context(nc.psum_tensor(name, [P, 512], F32))

        def sem(name):
            return ctx.enter_context(nc.semaphore(name))

        x1_dram = T["x1"]

        ident = sb("ident", [P, P])
        part_rows = sb("part_rows", [96, 2 * NS])
        spread = sb("spread", [96, 2 * NS, P], BF16)
        in_w = sb("in_w", [P, 4 * P])
        conv_w = [sb(f"conv_w{l}", [P, CH, TAPS]) for l in range(2)]
        conv_b = [sb(f"conv_b{l}", [P, CH]) for l in range(2)]
        x_w = sb("x_w", [P, CH, RANK + 2 * NS])
        dt_w = sb("dt_w", [RANK, CH * P])
        dt_b = [sb(f"dt_b{l}", [P, CH]) for l in range(2)]
        A = [sb(f"A{l}", [P, CH, NS]) for l in range(2)]
        skip_d = sb("skip_d", [P, CH])
        out_w = [sb(f"out_w{l}", [P, CH, DM]) for l in range(2)]
        sel_w = sb("sel_w", [P, E0])
        keys = sb("keys", [P, E0 * EH])
        values = sb("values", [P, 4, DM])
        route = sb("route", [P, 1])
        delta_w = sb("delta_w", [P, CH, CH * P])
        side_w = sb("side_w", [P, 4 * P])
        bc_w = sb("bc_w", [P, CH, 2 * NS])
        ln_g = sb("ln_g", [P, CH])
        ln_b = sb("ln_b", [P, CH])
        gain_sum = sb("gain_sum", [P, DM])
        bias_out = sb("bias_out", [P, DM])
        gate_w = sb("gate_w", [P, E1])
        gate_b = sb("gate_b", [P, E1])
        expert_bias = sb("expert_bias", [P, E1])
        before = sb("before", [P, P], BF16)
        ones = sb("ones", [P, P], BF16)
        tile_sizes = sb("tile_sizes", [P, E1, E1])
        tile_numbers = sb("tile_numbers", [P, BLOCKS, E1])
        idle = sb("idle", [P, 2])
        small = sb("small", [P, 4, 2 * NS])

        x_tok = sb("x_tok", [P, TILES, DM])
        x_back = sb("x_back", [P, TILES, DM])
        g_tok = [sb(f"g_tok{q}", [P, TILES, DM]) for q in range(2)]
        stats = sb("stats", [P, TILES, 6])
        mv = sb("mv", [P, TILES, 2])
        rstd = sb("rstd", [P, TILES])
        xnT = sb("xnT", [P, LEN])
        conv_in = sb("conv_in", [P, CH, LEN + TAPS])
        xl = [sb(f"xl{q}", [P, CH, LEN]) for q in range(2)]
        zs = [sb(f"zs{q}", [P, CH, LEN]) for q in range(2)]
        dt = [sb(f"dt{q}", [P, CH, LEN]) for q in range(2)]
        u = sb("u", [P, CH, LEN])
        sp_z0 = sb("sp_z", [P, LEN])
        sp_e0 = sb("sp_e", [P, LEN])
        sp_l0 = sb("sp_l", [P, LEN])
        xn = sp_z0[:, :].rearrange("p (j d) -> p j d", d=DM)
        dt_low = sb("dt_low", [RANK, LEN])
        parts = [sb(f"parts{q}", [96, LEN], BF16) for q in range(2)]
        rest = [u[0:2 * NS, t, 0:HALF] for t in range(2)]
        mid = [dt[q][0:2 * NS, 1, 0:HALF].bitcast(BF16) for q in range(2)]
        probs = sb("probs", [P, TILES, 24])
        replaced = sb("replaced", [P, TILES, 24])
        top = sb("top", [P, TILES, 8])
        wanted = sb("wanted", [P, TILES, 16])
        share = sb("share", [P, TILES, E0])
        share_sum = sb("share_sum", [P, TILES])
        ffn = sb("ffn", [P, 4, 512])
        scored = [ffn[:, j, :] for j in range(2)]
        scoredT = [ffn[:, 2 + j, :] for j in range(2)]
        sp_z = [sp_z0[:, :], ffn[:, 0:2, :].rearrange("p a b -> p (a b)")]
        sp_e = [sp_e0[:, :], ffn[:, 2:4, :].rearrange("p a b -> p (a b)")]
        sp_l = [sp_l0[:, :], x_tok[:, :, :].rearrange("p a b -> p (a b)")]
        sp_q = [conv_in[:, c, TAPS:TAPS + LEN] for c in range(CH)]
        expert = [sb(f"expert{j}", [P, 2 * FF + FB + DM]) for j in range(2)]
        block_x = [sb(f"block_x{j}", [P, DM]) for j in range(2)]
        block_xT = [sb(f"block_xT{j}", [P, P]) for j in range(2)]
        hidden = [keys, values[:, :, :].rearrange("p a b -> p (a b)")]
        block_y = [sb(f"block_y{j}", [P, DM]) for j in range(2)]
        onehot = sb("onehot", [P, TILES, E1], BF16)
        marks = sb("marks", [P, BLOCKS, E1])
        ones_e = sb("ones_e", [P, E1])
        zeros = block_y[0]
        blocks_of = sb("blocks_of", [P, E1])
        block_end = sb("block_end", [P, E1])
        first_slot = sb("first_slot", [P, E1])
        place = sb("place", [P, TILES, E1])
        place_sum = sb("place_sum", [P, TILES])
        expert_f = sb("expert_f", [P, BLOCKS])
        slot_of = [sb(f"slot_of{j}", [P, TILES], I32) for j in range(2)]
        block_expert = [sb(f"block_expert{j}", [P, BLOCKS], I32) for j in range(2)]

        decay = [sb(f"decay{j}", [P, CH, HALF]) for j in range(4)]
        inject = [sb(f"inject{j}", [P, CH, HALF]) for j in range(2)]
        hs = [sb(f"hs{j}", [P, CH, HALF]) for j in range(2)]
        c_sb = [sb(f"c_sb{j}", [P, HALF]) for j in range(2)]
        weighted = [sb(f"weighted{j}", [P, CH, HALF]) for j in range(4)]
        carry = sb("carry", [P, NS, CH])
        one_col = hs[0][:, :, 0:P]
        sum_tok = sp_l0[:, :].rearrange("p (j d) -> p j d", d=DM)
        out_stats = sb("out_stats", [P, TILES, 6])
        out_mv = sb("out_mv", [P, TILES, 2])
        out_r = sb("out_r", [P, TILES])
        out_nm = sb("out_nm", [P, TILES])

        b_ps = [pb(f"b_ps{j}") for j in range(2)]
        c_ps = pb("c_ps")
        y_ps = [pb(f"y_ps{c}") for c in range(CH)]
        side_ps = [pb(f"side_ps{j}") for j in range(3)]

        loaded = sem("loaded")
        prep = sem("prep")
        prep_act = sem("prep_act")
        prep_pe = sem("prep_pe")
        x_in, x_back_in = sem("x_in"), sem("x_back_in")
        expert_in = [sem(f"expert_in{j}") for j in range(2)]
        block_in = [sem(f"block_in{j}") for j in range(2)]
        block_out = [sem(f"block_out{j}") for j in range(2)]
        place_step, expert_step = sem("place_step"), sem("expert_step")
        slot_step = sem("slot_step")
        slots_ready, experts_ready = sem("slots_ready"), sem("experts_ready")
        zeroed, scattered, gathered = sem("zeroed"), sem("scattered"), sem("gathered")
        stored = sem("stored")
        b_ready, c_ready = sem("b_ready"), sem("c_ready")
        c_copied = sem("c_copied")
        decay_ready = sem("decay_ready")
        inject_ready = sem("inject_ready")
        scanned = sem("scanned")
        carried = sem("carried")
        weighted_ready = sem("weighted_ready")
        summed = sem("summed")
        y_taken = sem("y_taken")
        evac = sem("evac")
        full = [sem(f"side_full{j}") for j in range(3)]
        free = [sem(f"side_free{j}") for j in range(3)]
        back_sum = sem("back_sum")
        turned_stats = sem("turned_stats")
        ln_step = sem("ln_step")
        rstd_ready = sem("rstd_ready")
        conv_step = sem("conv_step")
        gate_step0, gate_step1 = sem("gate_step0"), sem("gate_step1")
        g_ready = sem("g_ready")
        silu_ready = sem("silu_ready")
        dt_low_ready = sem("dt_low_ready")
        hi_ready, mid_ready, mid_copied = sem("hi_ready"), sem("mid_ready"), sem("mid_copied")
        lo_ready = sem("lo_ready")
        sp_act, sp_dve = sem("sp_act"), sem("sp_dve")
        u_ready, u_rest = sem("u_ready"), sem("u_rest")
        back_step1, back_done = sem("back_step1"), sem("back_done")
        back_act = sem("back_act")

        FRONT = [
            [(4, "tr0", 0), (4, "tr1", 1), (5, "x00", 0), (5, "x01", 1), (5, "logits", 2), (6, "x10", 0), (6, "x11", 1),
             (7, "z00", 0), (7, "z01", 1), (7, "z10", 2), (8, "z11", 0)]
            + [(10 + j, f"score{j}", 0) for j in range(TILES)] + [(11 + j, f"turn{j}", 1) for j in range(TILES)]
            + [(12, "values0", 2), (16, "values1", 2)],
            [(4, "tr0", 0), (4, "tr1", 1), (8, "x00", 0), (8, "x01", 1), (9, "logits", 2), (10, "x10", 0), (10, "x11", 1)] + [(12, "ranks", 0),
             (15, "z00", 0), (15, "z01", 2), (16, "z10", 0), (16, "z11", 2)],
        ]
        FRONT[0] += [(19, "proj0", 0), (19, "proj1", 1), (22, "dt00", 2), (22, "dt01", 0), (25, "dt10", 1), (25, "dt11", 2)]
        FRONT[1] += [(21, "proj0", 2), (21, "proj1", 0), (23, "dt00", 1), (23, "dt01", 0), (26, "dt10", 0), (26, "dt11", 2)]
        BACK = [
            [(9, "out0", 1), (9, "out1", 2)],
            [(5, "turned0", 2), (5, "turned1", 0), (7, "turned2", 0), (7, "turned3", 2), (11, "out0", 2), (11, "out1", 0)],
        ]

        BLOCK = []
        for i in range(BLOCKS):
            BLOCK += [(2 * i, 2, f"T{i}", 2 if 2 * i == 20 else 1), (2 * i + 1, 2, f"H{i}", 1),
                      (2 * i + 2, 2, f"Y{i}", 1 if 2 * i + 2 == 22 else 2)]

        def layer_at(seq):
            return None if seq < 0 or seq >= 2 * SEQS else int(seq >= SEQS)

        def uses(like):
            b, f = layer_at(like - 1), layer_at(like + 1)
            U = [(k, 0, n, j) for k, n, j in (BACK[b] if b is not None else [])] \
                + [(k, 1, n, j) for k, n, j in (FRONT[f] if f is not None else [])]
            U += BLOCK if layer_at(like) == 1 else []
            return [(n, j) for k, _, n, j in sorted(U, key=lambda v: (v[0], v[1], v[1] == 2 and v[2][0] == "T"))]

        BANKS = {like: [[n for n, b in uses(like) if b == j] for j in range(3)] for like in range(-1, 2 * SEQS + 1)}
        BEFORE = {like: [sum(len(BANKS[m][j]) for m in range(-1, like)) for j in range(3)] for like in BANKS}

        def use(B, name):
            g, like = B
            j = [j for j in range(3) if name in BANKS[like][j]][0]
            n = BEFORE[like][j] + BANKS[like][j].index(name) + 1
            return j, n + (0 if isinstance(g, int) else (g - like) * len(BANKS[like][j]))

        def fill(pe, B, name):
            j, count = use(B, name)
            at_least(pe, free[j], count - 1)
            return side_ps[j], full[j]

        def taken(eng, B, name):
            j, count = use(B, name)
            eng.wait_ge(free[j], count)

        def take(eng, B, name):
            j, count = use(B, name)
            eng.wait_ge(full[j], count)
            return side_ps[j], free[j]

        def wait_apart(dve, sem, value):
            dve.wait_ge(sem, value)
            dve.tensor_copy(idle[:, 1:2], idle[:, 0:1])

        block = ctx.enter_context(nc.Block())

        N_LOADS = 0
        plain = [(ident, "ident"), (part_rows, "part_rows"), (in_w, "in_w"), (conv_w[0], "conv_w0"),
                 (conv_w[1], "conv_w1"), (conv_b[0], "conv_b0"), (conv_b[1], "conv_b1"), (x_w, "x_w"),
                 (dt_w, "dt_w"), (dt_b[0], "dt_b0"), (dt_b[1], "dt_b1"), (A[0], "A_log0"), (skip_d, "skip_d"),
                 (out_w[0], "out_w0"), (out_w[1], "out_w1"), (sel_w, "sel_w"), (keys, "keys"), (values, "values"),
                 (delta_w, "delta_w"), (bc_w, "bc_w"), (ln_g, "ln_g"),
                 (ln_b, "ln_b"), (gate_w, "gate_w"), (before, "before"), (ones, "ones")]
        spreads = [(route, "route", 1), (gate_b, "gate_b", E1), (expert_bias, "expert_bias", E1)]
        N_LOADS = 16 * (len(plain) + len(spreads) + 1)
        N_LOADS += 16 * 3

        x_src = [T["x"], x1_dram]
        x_dst = [x1_dram, out]

        def rows(ap, s):
            return ap.rearrange("(s j p) d -> s p j d", s=SEQS, p=P)[bass.ds(s, 1)].rearrange("a p j d -> p (a j) d")

        LAST_BACK = 19

        def sp_load_x(sp, layer, s, g):
            at_least(sp, u_ready, g)
            sp.dma_start(x_tok[:, :, :], rows(x_src[layer], s)).then_inc(x_in, 16)

        def sp_back(sp, layer, s, g, k):
            if k == 1:
                sp.wait_ge(stored, 16 * (g + 2))
                sp.dma_start(x_back[:, :, :], rows(x_src[layer], s)).then_inc(x_back_in, 16)
            if k == (12, 19)[layer]:
                sp.wait_ge(back_done, g + 1)
                sp.dma_start(rows(x_dst[layer], s), x_back[:, :, :]).then_inc(stored, 16)
        PER_BODY = [(BLOCKS + 1) // 2, BLOCKS // 2]

        def block_count(s, i):
            return PER_BODY[i % 2] * s + i // 2 + 1

        def sp_load_block(sp, B, s, par, i):
            j = i % 2
            if i == 0:
                sp.wait_ge(scattered, 16 * TILES * (s + 1))
            sp.dma_start(block_x[j][:, :], T[f"sorted_x{par}"][i * P:(i + 1) * P, :]).then_inc(block_in[j], 16)
            e = sp.value_load(block_expert[par][0:1, i:i + 1], min_val=0, max_val=E1 - 1)
            sp.dma_start(expert[j][:, :], T["experts"][bass.ds(e, 1)].rearrange("a p n -> p (a n)"))\
                .then_inc(expert_in[j], 16)

        def sp_blocks(sp, B, s, par, k):
            i = k // 2
            if k % 2 == 0 and 1 <= i <= BLOCKS:
                taken(sp, B, f"Y{i - 1}")
                sp.dma_start(T[f"sorted_y{par}"][(i - 1) * P:i * P, :], block_y[(i - 1) % 2][:, :])\
                    .then_inc(block_out[(i - 1) % 2], 16)
            if k % 2 == 0 and i + 1 < BLOCKS:
                sp_load_block(sp, B, s, par, i + 1)

        def pe_blocks(pe, B, s, k):
            i = k // 2
            if k % 2 == 0:
                if 1 <= i <= BLOCKS:
                    n = i - 1
                    taken(pe, B, f"H{n}")
                    bank, done = fill(pe, B, f"Y{n}")
                    for m in range(FB):
                        mm = pe.matmul(bank[:, 0:DM], hidden[n % 2][:, m * P:(m + 1) * P],
                                       expert[n % 2][:, FF + m * DM:FF + (m + 1) * DM], start=(m == 0), stop=(m == FB - 1))
                    mm.then_inc(done, 1)
                if i < BLOCKS:
                    pe.wait_ge(block_in[i % 2], 16 * block_count(s, i))
                    bank, done = fill(pe, B, f"T{i}")
                    pe.transpose(bank[:, 0:P], block_x[i % 2][:, :], ident[:, :]).then_inc(done, 1)
            elif i < BLOCKS:
                pe.wait_ge(expert_in[i % 2], 16 * block_count(s, i))
                taken(pe, B, f"T{i}")
                bank, done = fill(pe, B, f"H{i}")
                for m in range(FB):
                    mm = pe.matmul(bank[:, m * P:(m + 1) * P], expert[i % 2][:, m * P:(m + 1) * P], block_xT[i % 2][:, :],
                                   start=True, stop=True)
                mm.then_inc(done, 1)

        def act_blocks(act, B, s, k):
            i = k // 2
            if i >= BLOCKS:
                return
            if k % 2 == 0:
                bank, done = take(act, B, f"T{i}")
                act.activation(block_xT[i % 2][:, :], bank[:, 0:P], ACT.Copy).then_inc(done, 1)
            else:
                if i >= 2:
                    take(act, B, f"Y{i - 2}")
                bank, done = take(act, B, f"H{i}")
                for m in range(FB):
                    a = act.activation(hidden[i % 2][:, m * P:(m + 1) * P], bank[:, m * P:(m + 1) * P], ACT.Relu,
                                       bias=expert[i % 2][:, 2 * FF + m:2 * FF + m + 1])
                a.then_inc(done, 1)

        def dve_blocks(dve, B, s, k):
            i = k // 2 - 1
            if k % 2 == 0 and 0 <= i < BLOCKS:
                at_least(dve, block_out[i % 2], 16 * (block_count(s, i) - 1))
                bank, done = take(dve, B, f"Y{i}")
                dve.tensor_tensor(block_y[i % 2][:, :], bank[:, 0:DM], expert[i % 2][:, 2 * FF + FB:2 * FF + FB + DM],
                                  ALU.add).then_inc(done, 1)

        S_SCATTER, B_GATHER = 16, 1

        def pool_waits(pool, front, back, k):
            if front is not None and k == S_SCATTER:
                s = front
                pool.wait_ge(experts_ready, s + 1)
                pool.wait_ge(zeroed, 16 * 2 * (BLOCKS - 1))
                for j in range(2):
                    at_least(pool, block_in[j], 16 * PER_BODY[j] * (s - 1))
            if back is not None and k == B_GATHER:
                for j in range(2):
                    pool.wait_ge(block_out[j], 16 * PER_BODY[j] * (back + 1))

        def pool_indirect(pool, front, back, par, k):
            if front is not None and S_SCATTER <= k < S_SCATTER + TILES // 2:
                for n in range(2):
                    j = 2 * (k - S_SCATTER) + n
                    pool.indirect_dma_start(T[f"sorted_x{par}"], bass.IndirectOffsetOnAxis(slot_of[par][:, j:j + 1], 0),
                                            xn[:, j, :], None).then_inc(scattered, 16)
            if back is not None and B_GATHER <= k < B_GATHER + TILES // 2:
                for n in range(2):
                    j = 2 * (k - B_GATHER) + n
                    pool.indirect_dma_start(g_tok[par][:, j, :], None, T[f"sorted_y{par}"],
                                            bass.IndirectOffsetOnAxis(slot_of[par][:, j:j + 1], 0)).then_inc(gathered, 16)

        S_LOAD, S_STATS, S_RSTD, S_NORM, S_TURN = 0, 1, 2, 3, 4
        S_CONV, S_X = (10, 12), ((5, 6), (8, 10))
        S_GATE = (6, 10)
        S_Z, S_SILU, S_PROJ, S_REST, S_SP, S_U = (7, 15), (18, 20), (19, 21), (21, 22), (22, 23), (30, 30)
        S_FFN = 10

        def sp_front(sp, B, layer, s, g, q, k):
            if k == S_LOAD:
                sp_load_x(sp, layer, s, g)
            if layer == 1 and k == UNITS - 1:
                sp_load_block(sp, B, s, q, 0)

        def pe_front(pe, B, layer, s, g, q, k):
            if k == S_TURN:
                pe.wait_ge(ln_step, 3 * g + 3)
                for n in range(2):
                    bank, done = fill(pe, B, f"tr{n}")
                    for j in range(4):
                        mm = pe.transpose(bank[:, j * P:(j + 1) * P], xn[:, 4 * n + j, :], ident[:, :])
                    mm.then_inc(done, 1)
            w = in_w if layer == 0 else side_w
            for c in range(CH):
                if k == S_X[layer][c]:
                    if c == 0:
                        taken(pe, B, "tr0")
                        taken(pe, B, "tr1")
                    for t in range(2):
                        bank, done = fill(pe, B, f"x{c}{t}")
                        pe.matmul(bank[:, :], w[:, c * P:(c + 1) * P], xnT[:, t * HALF:(t + 1) * HALF],
                                  start=True, stop=True).then_inc(done, 1)
            if k == (5, 9)[layer]:
                bank, done = fill(pe, B, "logits")
                v, n = ((sel_w, E0), (gate_w, E1))[layer]
                for j in range(TILES):
                    mm = pe.matmul(bank[:, n * j:n * j + n], xnT[:, j * P:(j + 1) * P], v[:, :], start=True, stop=True)
                mm.then_inc(done, 1)
            for c in range(CH):
                for t in range(2):
                    if k == S_Z[layer] + (c + t == 2 or (layer == 1 and c == 1)):
                        bank, done = fill(pe, B, f"z{c}{t}")
                        pe.matmul(bank[:, :], w[:, (CH + c) * P:(CH + c + 1) * P], xnT[:, t * HALF:(t + 1) * HALF],
                                  start=True, stop=True).then_inc(done, 1)
            if layer == 0:
                j = k - S_FFN
                if 0 <= j < TILES:
                    bank, done = fill(pe, B, f"score{j}")
                    pe.matmul(bank[:, :], xnT[:, j * P:(j + 1) * P], keys[:, :], start=True, stop=True).then_inc(done, 1)
                j = k - S_FFN - 1
                if 0 <= j < TILES:
                    taken(pe, B, f"score{j}")
                    bank, done = fill(pe, B, f"turn{j}")
                    for m in range(4):
                        mm = pe.transpose(bank[:, m * P:(m + 1) * P], scored[j % 2][:, m * P:(m + 1) * P], ident[:, :])
                    mm.then_inc(done, 1)
                j = k - S_FFN - 2
                if 0 <= j < TILES:
                    taken(pe, B, f"turn{j}")
                    if j % 4 == 0:
                        bank, done = fill(pe, B, f"values{j // 4}")
                    else:
                        bank, done = side_ps[2], full[2]
                    for m in range(4):
                        mm = pe.matmul(bank[:, (j % 4) * DM:(j % 4 + 1) * DM], scoredT[j % 2][:, m * P:(m + 1) * P],
                                       values[:, m, :], start=(m == 0), stop=(m == 3))
                    mm.then_inc(value_done if j % 4 < 3 else done, 1)
            if layer == 1 and k == 12:
                pe.wait_ge(gate_step1, 5 * s + 5)
                bank, done = fill(pe, B, "ranks")
                pe.matmul(bank[:, 0:TILES * E1], before[:, :], onehot[:, :, :].rearrange("p j e -> p (j e)"),
                          start=True, stop=False)
                for j in range(TILES - 1):
                    n = TILES - 1 - j
                    pe.matmul(bank[:, (j + 1) * E1:TILES * E1], ones[:, :],
                              onehot[:, j, :].unsqueeze(1).to_broadcast([P, n, E1]), start=False, stop=(n == 1))
                for j in range(TILES):
                    mm = pe.matmul(bank[:, TILES * E1:(TILES + 1) * E1], ones[:, :], onehot[:, j, :],
                                   start=(j == 0), stop=(j == TILES - 1))
                mm.then_inc(done, 1)
            if k == S_PROJ[layer]:
                pe.wait_ge(silu_ready, g + 1)
                v, n = ((x_w, RANK + 2 * NS), (bc_w, 2 * NS))[layer]
                for t in range(2):
                    bank, done = fill(pe, B, f"proj{t}")
                    for c in range(CH):
                        mm = pe.matmul(bank[0:n, :], v[:, c, :], xl[q][:, c, t * HALF:(t + 1) * HALF],
                                       start=(c == 0), stop=(c == CH - 1))
                    mm.then_inc(done, 1)
            if k in (S_SP[layer], S_SP[layer] + 3):
                c = (k - S_SP[layer]) // 3
                if layer == 0:
                    pe.wait_ge(dt_low_ready, 2 * s + 2)
                for t in range(2):
                    bank, done = fill(pe, B, f"dt{c}{t}")
                    if layer == 0:
                        mm = pe.matmul(bank[:, :], dt_w[:, c * P:(c + 1) * P], dt_low[:, t * HALF:(t + 1) * HALF],
                                       start=True, stop=True)
                    else:
                        for i in range(CH):
                            mm = pe.matmul(bank[:, :], delta_w[:, i, c * P:(c + 1) * P],
                                           xl[q][:, i, t * HALF:(t + 1) * HALF], start=(i == 0), stop=(i == CH - 1))
                    mm.then_inc(done, 1)

        value_done = sem("value_done")

        def value_read(eng, B, s, j):
            if j % 4 == 3:
                take(eng, B, f"values{j // 4}")
            else:
                eng.wait_ge(value_done, 3 * (TILES // 4) * s + 3 * (j // 4) + j % 4 + 1)

        def act_front(act, B, layer, s, g, q, k):
            if k == S_RSTD:
                act.wait_ge(ln_step, 3 * g + 2)
                act.activation(rstd[:, :], rstd[:, :], ACT.Ln).then_inc(rstd_ready, 1)
                act.wait_ge(rstd_ready, 2 * g + 1)
                act.activation(rstd[:, :], rstd[:, :], ACT.Exp, scale=-0.5).then_inc(rstd_ready, 1)
            if k == S_TURN:
                for n in range(2):
                    bank, done = take(act, B, f"tr{n}")
                    act.activation(xnT[:, n * HALF:(n + 1) * HALF], bank[:, :], ACT.Copy).then_inc(done, 1)
            for c in range(CH):
                if k == S_X[layer][c]:
                    if c == 0:
                        at_least(act, u_ready, g)
                    for t in range(2):
                        bank, done = take(act, B, f"x{c}{t}")
                        act.activation(conv_in[:, c, TAPS - 1 + t * HALF:TAPS - 1 + (t + 1) * HALF], bank[:, :],
                                       ACT.Copy).then_inc(done, 1)
            if layer == 0 and k == 5:
                bank, done = take(act, B, "logits")
                act.activation(probs[:, :, 0:E0], bank[:, 0:TILES * E0].rearrange("p (j e) -> p j e", e=E0),
                               ACT.Exp, scale=-1.0).then_inc(done, 1)
            if layer == 0:
                j = k - S_FFN - 1
                if 0 <= j < TILES:
                    bank, done = take(act, B, f"turn{j}")
                    if j >= 2:
                        value_read(act, B, s, j - 2)
                    act.activation(scoredT[j % 2], bank[:, :], ACT.Copy).then_inc(done, 1)
                j = k - S_FFN - 2
                if 0 <= j < TILES and j % 4 == 3:
                    j0 = j - 3
                    bank, done = take(act, B, f"values{j // 4}")
                    if j0 == 0:
                        at_least(act, back_done, s - 1)
                    act.activation(g_tok[q][:, j0:j0 + 4, :], bank[:, :].rearrange("p (j d) -> p j d", d=DM),
                                   ACT.Copy).then_inc(done, 1)
            if k == S_REST[layer] + 1:
                for t in range(2):
                    cols = slice(t * HALF, (t + 1) * HALF)
                    taken(act, B, f"proj{t}")
                    act.activation(mid[q][:, cols], rest[t], ACT.Copy).then_inc(mid_ready, 1)
                    act.wait_ge(mid_ready, 2 * g + t + 1)
                    act.activation(parts[q][2 * NS:4 * NS, cols], mid[q][:, cols], ACT.Copy).then_inc(mid_copied, 1)
            if k in (S_SP[layer], S_SP[layer] + 3):
                c = (k - S_SP[layer]) // 3
                n = 4 * (CH * g + c)
                if layer == 1 and c == 0:
                    act.wait_ge(scattered, 16 * TILES * (s + 1))
                for t in range(2):
                    bank, done = take(act, B, f"dt{c}{t}")
                    act.activation(sp_z[c][:, t * HALF:(t + 1) * HALF], bank[:, :], ACT.Identity,
                                   bias=dt_b[layer][:, c:c + 1]).then_inc(done, 1)
                taken(act, B, f"dt{c}0")
                taken(act, B, f"dt{c}1")
                act.activation(sp_e[c], sp_z[c], ACT.Abs).then_inc(sp_act, 1)
            if k in (S_SP[layer] + 1, S_SP[layer] + 4):
                c = (k - S_SP[layer] - 1) // 3
                n = 4 * (CH * g + c)
                act.wait_ge(sp_act, n + 1)
                act.activation(sp_e[c], sp_e[c], ACT.Exp, scale=-1.0).then_inc(sp_act, 1)
                act.wait_ge(sp_act, n + 2)
                if c == 1:
                    act.wait_ge(lo_ready, 2 * g + 2)
                act.activation(dt[q][:, c, :], sp_e[c], ACT.Copy, bias=1.0).then_inc(sp_act, 1)
            if k in (S_SP[layer] + 2, S_SP[layer] + 5):
                c = (k - S_SP[layer] - 2) // 3
                n = 4 * (CH * g + c)
                if c == 0:
                    at_least(act, back_done, B[0])
                act.wait_ge(sp_act, n + 3)
                act.activation(sp_l[c], dt[q][:, c, :], ACT.Ln).then_inc(sp_act, 1)
                if layer == 0:
                    act.activation(sp_q[c], sp_e[c], ACT.Square, scale=0.5 ** 0.5).then_inc(square_ready, 1)
            if k == S_Z[layer]:
                if layer == 0:
                    at_least(act, evac, 2 * (g - 1))
                for c in range(CH):
                    for t in range(2):
                        bank, done = take(act, B, f"z{c}{t}")
                        act.activation(zs[q][:, c, t * HALF:(t + 1) * HALF], bank[:, :], ACT.Silu).then_inc(done, 1)
                nc.scalar.preload_act_table_set(EXP_LN)
            if k == S_SILU[layer]:
                act.wait_ge(conv_step, 8 * g + 8)
                for c in range(CH):
                    i = act.activation(xl[q][:, c, :], xl[q][:, c, :], ACT.Silu, bias=conv_b[layer][:, c:c + 1])
                i.then_inc(silu_ready, 1)
                nc.scalar.preload_act_table_set(EXP_LN)
            if k == S_PROJ[layer]:
                r = RANK if layer == 0 else 0
                for t in range(2):
                    cols = slice(t * HALF, (t + 1) * HALF)
                    bank, _ = take(act, B, f"proj{t}")
                    if layer == 0:
                        act.activation(dt_low[:, cols], bank[0:RANK, :], ACT.Copy).then_inc(dt_low_ready, 1)
                    if t == 0:
                        at_least(act, c_ready, UNITS * (g - 1))
                    act.activation(parts[q][0:2 * NS, cols], bank[r:r + 2 * NS, :], ACT.Copy).then_inc(hi_ready, 1)

        def dve_front(dve, B, layer, s, g, q, k):
            if k == S_STATS:
                dve.wait_ge(x_in, 16 * (g + 1))
                for j in range(TILES):
                    i = dve.bn_stats(stats[:, j, :], x_tok[:, j, :])
                i.then_inc(ln_step, 1)
                wait_apart(dve, ln_step, 3 * g + 1)
                for j in range(TILES):
                    i = dve.bn_aggr(mv[:, j, :], stats[:, j, :])
                i.then_inc(ln_extra, 1)
                dve.wait_ge(ln_extra, g + 1)
                dve.tensor_scalar(rstd[:, :], mv[:, :, 1], EPS, None, ALU.add).then_inc(ln_step, 1)
            if k == S_NORM:
                dve.wait_ge(rstd_ready, 2 * g + 2)
                for j in range(TILES):
                    i = dve.tensor_scalar(xn[:, j, :], x_tok[:, j, :], mv[:, j, 0:1], rstd[:, j:j + 1],
                                          ALU.subtract, ALU.mult)
                i.then_inc(ln_step, 1)
            if S_CONV[layer] <= k < S_CONV[layer] + 2 * TAPS:
                c, tap = divmod(k - S_CONV[layer], TAPS)
                src = conv_in[:, c, tap:tap + LEN]
                w = conv_w[layer][:, c, tap:tap + 1]
                if tap == 0:
                    taken(dve, B, f"x{c}0")
                    taken(dve, B, f"x{c}1")
                    if layer_at(B[1] - 1) == 1:
                        for n in range(2):
                            j, cnt = use(B, f"out{n}")
                            dve.wait_ge(full[j], cnt)
                    dve.tensor_scalar(xl[q][:, c, :], src, w, None, ALU.mult).then_inc(conv_step, 1)
                else:
                    dve.wait_ge(conv_step, 8 * g + TAPS * c + tap)
                    dve.scalar_tensor_tensor(xl[q][:, c, :], src, w, xl[q][:, c, :], ALU.mult,
                                             ALU.add).then_inc(conv_step, 1)
            if layer == 0 and k == S_GATE[0]:
                n = 9 * s
                taken(dve, B, "logits")
                dve.tensor_scalar(replaced[:, :, 0:E0], probs[:, :, 0:E0], 1.0, None, ALU.add).then_inc(gate_step0, 1)
                dve.wait_ge(gate_step0, n + 1)
                dve.reciprocal(probs[:, :, 0:E0], replaced[:, :, 0:E0]).then_inc(gate_step0, 1)
                wait_apart(dve, gate_step0, n + 2)
                for j in range(TILES):
                    i = dve.max(top[:, j, :], probs[:, j, 0:E0])
                i.then_inc(gate_step0, 1)
                dve.wait_ge(gate_step0, n + 3)
                dve.tensor_copy(wanted[:, :, 0:K0], top[:, :, 0:K0]).then_inc(gate_step0, 1)
            if layer == 0 and k == S_GATE[0] + 1:
                n = 9 * s
                wait_apart(dve, gate_step0, n + 4)
                for j in range(TILES):
                    i = dve.match_replace(replaced[:, j, 0:E0 + 8 - K0], wanted[:, j, 0:8],
                                          probs[:, j, 0:E0 + 8 - K0], -1.0)
                i.then_inc(gate_step0, 1)
                dve.wait_ge(gate_step0, n + 5)
                dve.scalar_tensor_tensor(share[:, :, :], replaced[:, :, 0:E0], 0.0, probs[:, :, 0:E0], ALU.is_lt,
                                         ALU.mult).then_inc(gate_step0, 1)
                dve.wait_ge(gate_step0, n + 6)
                dve.tensor_reduce(share_sum[:, :], share[:, :, :], AX.X, ALU.add).then_inc(gate_step0, 1)
                dve.wait_ge(gate_step0, n + 7)
                dve.tensor_scalar(share_sum[:, :], share_sum[:, :], 1e-9, None, ALU.max).then_inc(gate_extra, 1)
                dve.wait_ge(gate_extra, 2 * s + 1)
                dve.reciprocal(share_sum[:, :], share_sum[:, :]).then_inc(gate_step0, 1)
                dve.wait_ge(gate_step0, n + 8)
                dve.tensor_scalar(share_sum[:, :], share_sum[:, :], route[:, 0:1], None, ALU.mult).then_inc(gate_extra, 1)
                dve.wait_ge(gate_extra, 2 * s + 2)
                dve.tensor_tensor(share[:, :, :], share[:, :, :],
                                  share_sum[:, :].unsqueeze(2).to_broadcast([P, TILES, E0]), ALU.mult).then_inc(gate_step0, 1)
            if layer == 0 and S_FFN <= k < S_FFN + TILES:
                j = k - S_FFN
                if j == 0:
                    dve.wait_ge(gate_step0, 9 * s + 9)
                bank, done = take(dve, B, f"score{j}")
                if j >= 2:
                    jt, cnt = use(B, f"turn{j - 2}")
                    dve.wait_ge(full[jt], cnt)
                dve.scalar_tensor_tensor(scored[j % 2].rearrange("p (e h) -> p e h", h=EH),
                                         bank[:, :].rearrange("p (e h) -> p e h", h=EH), 0.0,
                                         share[:, j, :].unsqueeze(2).to_broadcast([P, E0, EH]),
                                         ALU.max, ALU.mult).then_inc(done, 1)
            if layer == 1 and k == S_GATE[1]:
                n = 5 * s
                bank, done = take(dve, B, "logits")
                logits = probs[:, :, E1:2 * E1]
                dve.tensor_tensor(logits, bank[:, 0:TILES * E1].rearrange("p (j e) -> p j e", e=E1),
                                  gate_b[:, :].unsqueeze(1).to_broadcast([P, TILES, E1]), ALU.add).then_inc(done, 1)
                taken(dve, B, "logits")
                dve.tensor_tensor(logits, logits,
                                  expert_bias[:, :].unsqueeze(1).to_broadcast([P, TILES, E1]), ALU.add).then_inc(gate_step1, 1)
                wait_apart(dve, gate_step1, n + 1)
                for j in range(TILES):
                    i = dve.max(top[:, j, :], probs[:, j, E1:2 * E1])
                i.then_inc(gate_step1, 1)
                dve.wait_ge(gate_step1, n + 2)
                dve.tensor_copy(wanted[:, :, 8:9], top[:, :, 0:1]).then_inc(gate_step1, 1)
            if layer == 1 and k == S_GATE[1] + 1:
                n = 5 * s
                wait_apart(dve, gate_step1, n + 3)
                for j in range(TILES):
                    i = dve.match_replace(replaced[:, j, 0:2 * E1 - 1], wanted[:, j, 8:16], probs[:, j, E1:3 * E1 - 1],
                                          -SENTINEL)
                i.then_inc(gate_step1, 1)
                dve.wait_ge(gate_step1, n + 4)
                dve.tensor_scalar(onehot[:, :, :], replaced[:, :, 0:E1], -SENTINEL, None, ALU.is_le).then_inc(gate_step1, 1)
            for c in range(CH):
                n = 3 * (CH * g + c)
                d = dt[q][:, c, :]
                if k == 26 + 3 * c:
                    dve.wait_ge(sp_act, 4 * (CH * g + c) + 4)
                    dve.scalar_tensor_tensor(d, d, -1.0, sp_e[c], ALU.add, ALU.subtract).then_inc(sp_dve, 1)
                    dve.wait_ge(sp_dve, n + 1)
                    dve.tensor_tensor(d, sp_l[c], d, ALU.subtract).then_inc(sp_dve, 1)
                if k == 27 + 3 * c:
                    if layer == 0:
                        dve.wait_ge(square_ready, CH * s + c + 1)
                        dve.tensor_tensor(sp_q[c], sp_e[c], sp_q[c], ALU.subtract).then_inc(series_ready, 1)
                        dve.wait_ge(series_ready, CH * s + c + 1)
                        dve.wait_ge(sp_dve, n + 2)
                        dve.scalar_tensor_tensor(d, d, -LN_ERROR, sp_q[c], ALU.add, ALU.max).then_inc(lowered, 1)
                        dve.wait_ge(lowered, CH * s + c + 1)
                    else:
                        dve.wait_ge(sp_dve, n + 2)
                    dve.scalar_tensor_tensor(d, sp_z[c], 0.0, d, ALU.max, ALU.add).then_inc(sp_dve, 1)
                    if layer == 1:
                        dve.wait_ge(sp_dve, n + 3)
                        dve.tensor_scalar(d, d, 1e-4, 10.0, ALU.max, ALU.min).then_inc(clipped, 1)
            if layer == 1 and k == 13:
                n = 4 * s
                bank, _ = take(dve, B, "ranks")
                dve.tensor_tensor(marks[:, 0:E1, :], bank[:, TILES * E1:(TILES + 1) * E1].unsqueeze(2)
                                  .to_broadcast([P, E1, E1]), tile_sizes[:, :, :], ALU.is_gt).then_inc(slot_step, 1)
                dve.wait_ge(slot_step, n + 1)
                dve.tensor_reduce(blocks_of[:, :], marks[:, 0:E1, :], AX.X, ALU.add).then_inc(slot_step, 1)
                dve.wait_ge(slot_step, n + 2)
                dve.tensor_tensor_scan(block_end[:, :], ones_e[:, :], blocks_of[:, :], 0.0, ALU.mult,
                                       ALU.add).then_inc(slot_step, 1)
                dve.wait_ge(slot_step, n + 3)
                dve.tensor_tensor(first_slot[:, :], block_end[:, :], blocks_of[:, :], ALU.subtract).then_inc(slot_step, 1)
            if layer == 1 and k == 14:
                n = 4 * s
                bank, done = take(dve, B, "ranks")
                dve.wait_ge(slot_step, n + 4)
                dve.scalar_tensor_tensor(place[:, :, :], first_slot[:, :].unsqueeze(1).to_broadcast([P, TILES, E1]), float(P),
                                         bank[:, 0:TILES * E1].rearrange("p (j e) -> p j e", e=E1), ALU.mult,
                                         ALU.add).then_inc(done, 1)
                taken(dve, B, "ranks")
                dve.tensor_tensor(place[:, :, :], place[:, :, :], onehot[:, :, :], ALU.mult).then_inc(place_step, 1)
                dve.wait_ge(place_step, 2 * s + 1)
                dve.tensor_reduce(place_sum[:, :], place[:, :, :], AX.X, ALU.add).then_inc(place_step, 1)
                dve.wait_ge(place_step, 2 * s + 2)
                at_least(dve, gathered, 16 * TILES * (s - 1))
                dve.tensor_copy(slot_of[q][:, :], place_sum[:, :]).then_inc(slots_ready, 1)
            if layer == 1 and k == 15:
                n = 3 * s
                dve.tensor_tensor(marks[:, :, :], block_end[:, :].unsqueeze(1).to_broadcast([P, BLOCKS, E1]),
                                  tile_numbers[:, :, :], ALU.is_le).then_inc(expert_step, 1)
                dve.wait_ge(expert_step, 2 * s + 1)
                dve.tensor_reduce(expert_f[:, :], marks[:, :, :], AX.X, ALU.add).then_inc(expert_step, 1)
                dve.wait_ge(expert_step, 2 * s + 2)
                for j in range(2):
                    at_least(dve, expert_in[j], 16 * PER_BODY[j] * (s - 1))
                dve.tensor_scalar(block_expert[q][:, :], expert_f[:, :], float(E1 - 1), None, ALU.min)\
                    .then_inc(experts_ready, 1)
            if k == S_REST[layer]:
                r = RANK if layer == 0 else 0
                for t in range(2):
                    cols = slice(t * HALF, (t + 1) * HALF)
                    bank, done = take(dve, B, f"proj{t}")
                    dve.wait_ge(hi_ready, 2 * g + t + 1)
                    dve.tensor_tensor(rest[t], bank[r:r + 2 * NS, :], parts[q][0:2 * NS, cols],
                                      ALU.subtract).then_inc(done, 1)
            if k == S_REST[layer] + 2:
                for t in range(2):
                    cols = slice(t * HALF, (t + 1) * HALF)
                    taken(dve, B, f"proj{t}")
                    dve.wait_ge(mid_ready, 2 * g + t + 1)
                    dve.tensor_tensor(parts[q][4 * NS:6 * NS, cols], rest[t], mid[q][:, cols],
                                      ALU.subtract).then_inc(lo_ready, 1)
            if k == S_U[layer]:
                dve.wait_ge(sp_dve, 3 * CH * (g + 1))
                if layer == 1:
                    dve.wait_ge(clipped, CH * (s + 1))
                dve.wait_ge(silu_ready, g + 1)
                dve.wait_ge(mid_ready, 2 * g + 2)
                dve.wait_ge(lo_ready, 2 * g + 2)
                dve.tensor_tensor(u[:, :, 0:HALF], dt[q][:, :, 0:HALF], xl[q][:, :, 0:HALF], ALU.mult).then_inc(u_ready, 1)

        ln_extra = sem("ln_extra")
        gate_extra = sem("gate_extra")
        clipped = sem("clipped")
        square_ready, series_ready, lowered = sem("square_ready"), sem("series_ready"), sem("lowered")

        def unit(g, k, lag):
            if k - lag >= UNITS:
                return g + 1, k - lag - UNITS
            return (g, k - lag) if k >= lag else (g - 1, k - lag + UNITS)

        def none(g, k):
            return isinstance(g, int) and (g < 0 or g >= 2 * SEQS)

        def count(g, k):
            return g * UNITS + (k + 1)

        def pe_core(pe, g, k, p):
            if not none(g, k):
                tc, n = divmod(k, NS)
                cols = slice(tc * HALF, (tc + 1) * HALF)
                at_least(pe, c_copied, count(g, k) - 1)
                pe.matmul(c_ps[:, :], spread[:, NS + n, :], parts[p][:, cols], start=True, stop=True).then_inc(c_ready, 1)
            gb, kb = unit(g, k, -1)
            if not none(gb, kb):
                side = p if kb else 1 - p
                tc, n = divmod(kb, NS)
                cols = slice(tc * HALF, (tc + 1) * HALF)
                if kb == 0:
                    pe.wait_ge(hi_ready, 2 * gb + 2)
                    pe.wait_ge(mid_copied, 2 * gb + 2)
                    pe.wait_ge(lo_ready, 2 * gb + 2)
                at_least(pe, inject_ready, count(gb, kb) - 2)
                pe.matmul(b_ps[kb % 2][:, :], spread[:, n, :], parts[side][:, cols], start=True, stop=True).then_inc(b_ready, 1)
            gr, kr = unit(g, k, R_LAG)
            if not none(gr, kr):
                for ks in {0: (), 1: (kr - 1, kr)}.get(kr % NS, (kr,)):
                    tc, n = divmod(ks, NS)
                    pe.wait_ge(weighted_ready, count(gr, ks))
                    if n == 0:
                        at_least(pe, y_taken, gr * 2 + tc)
                    for c in range(CH):
                        mm = pe.matmul(y_ps[c][:, :], ident[:, :], weighted[ks % 4][:, c, :], start=(n == 0),
                                       stop=(n == NS - 1))
                    mm.then_inc(summed, 1)

        def act_core(act, g, k, p, like):
            if not none(g, k):
                act.wait_ge(c_ready, count(g, k))
                at_least(act, weighted_ready, count(g, k) - 2)
                act.activation(c_sb[k % 2][:, :], c_ps[:, :], ACT.Copy).then_inc(c_copied, 1)
            ga, ka = unit(g, k, -2)
            if not none(ga, ka) and not (like == -1 and k < UNITS - 2):
                layer = layer_at(like if ka > 1 else like + 1)
                tc, n = divmod(ka, NS)
                cols = slice(tc * HALF, (tc + 1) * HALF)
                at_least(act, scanned, count(ga, ka) - 4)
                if ka == 0:
                    act.wait_ge(u_ready, ga + 1)
                for c in range(CH):
                    i = act.activation(decay[ka % 4][:, c, :], dt[p if ka > 1 else 1 - p][:, c, cols], ACT.Exp,
                                       scale=A[layer][:, c, n:n + 1])
                i.then_inc(decay_ready, 1)

        def dve_core(dve, g, k, p):
            if not none(g, k):
                tc, n = divmod(k, NS)
                cols = slice(tc * HALF, (tc + 1) * HALF)
                if k == 0:
                    dve.wait_ge(u_ready, g + 1)
                if k == NS:
                    dve.wait_ge(u_rest, g + 1)
                dve.wait_ge(b_ready, count(g, k))
                at_least(dve, scanned, count(g, k) - 2)
                dve.tensor_tensor(inject[k % 2][:, :, :], u[:, :, cols],
                                  b_ps[k % 2][:, :].unsqueeze(1).to_broadcast([P, CH, HALF]), ALU.mult).then_inc(inject_ready, 1)
            gs, ks = unit(g, k, 1)
            if not none(gs, ks):
                tc, n = divmod(ks, NS)
                dve.wait_ge(inject_ready, count(gs, ks))
                dve.wait_ge(decay_ready, count(gs, ks))
                at_least(dve, weighted_ready, count(gs, ks) - 2)
                if ks < NS + 2:
                    at_least(dve, carried, gs * NS + ks - 1)
                for c in range(CH):
                    i = dve.tensor_tensor_scan(hs[ks % 2][:, c, :], decay[ks % 4][:, c, :], inject[ks % 2][:, c, :],
                                               carry[:, n, c:c + 1] if tc else 0.0, ALU.mult, ALU.add)
                i.then_inc(scanned, 1)

        def pool_core(pool, g, k):
            if none(g, k):
                return
            tc, n = divmod(k, NS)
            pool.wait_ge(scanned, count(g, k))
            pool.wait_ge(c_copied, count(g, k))
            at_least(pool, summed, count(g, k) - 4)
            pool.tensor_tensor(weighted[k % 4][:, :, :], hs[k % 2][:, :, :],
                               c_sb[k % 2][:, :].unsqueeze(1).to_broadcast([P, CH, HALF]), ALU.mult).then_inc(weighted_ready, 1)
            if tc == 0:
                pool.tensor_copy(carry[:, n, :], hs[k % 2][:, :, HALF - 1]).then_inc(carried, 1)

        def pool_u(pool, g, p):
            pool.tensor_tensor(u[:, :, HALF:LEN], dt[p][:, :, HALF:LEN], xl[p][:, :, HALF:LEN], ALU.mult).then_inc(u_rest, 1)

        def dve_gate_y(dve, g, tc, p):
            cols = slice(tc * HALF, (tc + 1) * HALF)
            dve.wait_ge(y_taken, 2 * g + tc + 1)
            dve.tensor_tensor(xl[p][:, :, cols], xl[p][:, :, cols], zs[p][:, :, cols], ALU.mult).then_inc(evac, 1)

        def dve_take_y(dve, g, tc, p, layer):
            cols = slice(tc * HALF, (tc + 1) * HALF)
            dve.wait_ge(summed, count(g, tc * NS + NS - 1))
            if layer == 0:
                for c in range(CH):
                    i = dve.scalar_tensor_tensor(xl[p][:, c, cols], xl[p][:, c, cols], skip_d[:, c:c + 1],
                                                 y_ps[c][:, :], ALU.mult, ALU.add)
                i.then_inc(y_taken, 1)
            else:
                for c in range(CH):
                    i = dve.tensor_tensor(xl[p][:, c, cols], zs[p][:, c, cols], y_ps[c][:, :], ALU.mult)
                i.then_inc(y_taken, 1)

        def pe_back(pe, B, layer, s, g, p, k):
            if k == (9, 11)[layer]:
                if layer == 0:
                    pe.wait_ge(evac, 2 * g + 2)
                for n in range(2):
                    bank, done = fill(pe, B, f"out{n}")
                    for j in range(4):
                        cols = slice((4 * n + j) * P, (4 * n + j + 1) * P)
                        for c in range(CH):
                            mm = pe.matmul(bank[:, j * DM:(j + 1) * DM], xl[p][:, c, cols], out_w[layer][:, c, :],
                                           start=(c == 0), stop=(c == CH - 1))
                    mm.then_inc(done, 1)
            if layer == 1 and k in (5, 7):
                if k == 5:
                    pe.wait_ge(y_taken, 2 * g + 2)
                for n in (0, 1) if k == 5 else (2, 3):
                    bank, done = fill(pe, B, f"turned{n}")
                    for j in range(2):
                        for c in range(CH):
                            mm = pe.transpose(bank[:, (2 * j + c) * P:(2 * j + c + 1) * P],
                                              xl[p][:, c, (2 * n + j) * P:(2 * n + j + 1) * P], ident[:, :])
                    mm.then_inc(done, 1)

        def dve_back(dve, B, layer, s, g, p, k):
            if layer == 0 and k == (9 if layer_at(B[1] + 1) == 1 else 10):
                dve.wait_ge(g_ready, g + 1)
                for n in range(2):
                    tiles = slice(4 * n, 4 * n + 4)
                    bank, done = take(dve, B, f"out{n}")
                    dve.tensor_tensor(sum_tok[:, tiles, :], bank[:, :].rearrange("p (j d) -> p j d", d=DM),
                                      g_tok[p][:, tiles, :], ALU.mult).then_inc(done, 1)
            if layer == 1 and k in (6, 8):
                for n in (0, 1) if k == 6 else (2, 3):
                    bank, done = take(dve, B, f"turned{n}")
                    for j in range(2):
                        i = dve.bn_stats(out_stats[:, 2 * n + j, :], bank[:, 2 * j * P:2 * (j + 1) * P])
                    i.then_inc(done, 1)
            if layer == 1 and k == 8:
                for n in range(4):
                    taken(dve, B, f"turned{n}")
                dve.tensor_copy(idle[:, 1:2], idle[:, 0:1])
                for j in range(TILES):
                    i = dve.bn_aggr(out_mv[:, j, :], out_stats[:, j, :])
                i.then_inc(back_step1, 1)
                dve.wait_ge(back_step1, 4 * s + 1)
                dve.tensor_scalar(out_r[:, :], out_mv[:, :, 1], EPS, None, ALU.add).then_inc(back_step1, 1)
            if layer == 1 and k == 10:
                dve.wait_ge(back_act, 2 * s + 2)
                dve.scalar_tensor_tensor(out_nm[:, :], out_mv[:, :, 0], -1.0, out_r[:, :], ALU.mult, ALU.mult)\
                    .then_inc(back_step1, 1)
                dve.wait_ge(back_step1, 4 * s + 3)
                for j in range(TILES):
                    i = dve.scalar_tensor_tensor(sum_tok[:, j, :], gain_sum[:, :], out_nm[:, j:j + 1], bias_out[:, :],
                                                 ALU.mult, ALU.add)
                i.then_inc(back_sum, 1)
            for n in range(2 if layer == 1 and k == 12 else 0):
                if n == 0:
                    dve.wait_ge(back_sum, s + 1)
                bank, done = take(dve, B, f"out{n}")
                for j in range(4):
                    m = 4 * n + j
                    i = dve.scalar_tensor_tensor(sum_tok[:, m, :], bank[:, j * DM:(j + 1) * DM],
                                                 out_r[:, m:m + 1], sum_tok[:, m, :], ALU.mult, ALU.add)
                i.then_inc(done, 1)
            if layer == 1 and k == 17:
                taken(dve, B, "out0")
                taken(dve, B, "out1")
                dve.wait_ge(g_ready, g + 1)
                dve.tensor_tensor(sum_tok[:, :, :], sum_tok[:, :, :], g_tok[p][:, :, :], ALU.mult).then_inc(back_step1, 1)

        def pool_back(pool, B, layer, s, g, k):
            if k == (11, 18)[layer]:
                if layer == 0:
                    taken(pool, B, "out0")
                    taken(pool, B, "out1")
                else:
                    pool.wait_ge(back_step1, 4 * s + 4)
                pool.wait_ge(x_back_in, 16 * (g + 1))
                pool.tensor_tensor(x_back[:, :, :], x_back[:, :, :], sum_tok[:, :, :], ALU.add).then_inc(back_done, 1)

        def act_back(act, B, layer, s, g, p, k):
            if k == S_Z[layer]:
                if layer == 1:
                    act.wait_ge(gathered, 16 * TILES * (s + 1))
                act.activation(g_tok[p][:, :, :], g_tok[p][:, :, :], ACT.Silu).then_inc(g_ready, 1)
                if layer_at(B[1] + 1) != layer:
                    nc.scalar.preload_act_table_set(EXP_LN)
            if layer == 1 and k == 9:
                act.wait_ge(back_step1, 4 * s + 2)
                act.activation(out_r[:, :], out_r[:, :], ACT.Ln).then_inc(back_act, 1)
                act.wait_ge(back_act, 2 * s + 1)
                act.activation(out_r[:, :], out_r[:, :], ACT.Exp, scale=-0.5).then_inc(back_act, 1)

        def layer_of(g, static):
            return 0 if static < SEQS else 1

        def over_bodies(eng, body):
            body(-1, -1)
            body(0, 0)
            for layer in range(2):
                first = SEQS * layer + 1
                with eng.Fori(0, (SEQS - 2) // 2) as i:
                    for m in range(2):
                        body(first + m + 2 * i, first + m)
                body(SEQS * layer + SEQS - 1, SEQS * layer + SEQS - 1)
                if layer == 0:
                    body(SEQS, SEQS)
            body(2 * SEQS, 2 * SEQS)

        def local(g, like):
            return (0, g) if like < SEQS else (1, g - SEQS)

        @block.sync
        def _(sp):
            for dst, name in plain[0::2]:
                sp.dma_start(dst[:], T[name]).then_inc(loaded, 16)
            sp.dma_start(side_w[:, :], T["side_w"]).then_inc(loaded, 16)
            for dst, name, n in ((tile_sizes, "tile_sizes", E1 * E1), (tile_numbers, "tile_numbers", BLOCKS * E1)):
                sp.dma_start(dst[:, :, :].rearrange("p a b -> p (a b)"),
                             T[name].rearrange("(a n) -> a n", a=1).to_broadcast([P, n])).then_inc(loaded, 16)
            for dst, name, n in spreads:
                sp.dma_start(dst[:, :], T[name].rearrange("(a n) -> a n", a=1).to_broadcast([P, n])).then_inc(loaded, 16)
            sp.dma_start(A[1][:, 0, :], T["A_log1"].rearrange("(a n) -> a n", a=1).to_broadcast([P, NS])).then_inc(loaded, 16)

            def zero_padding():
                sp.wait_ge(prep, PREP_ZERO)
                for j in range(2):
                    for i in range(BLOCKS):
                        sp.dma_start(T[f"sorted_x{j}"][i * P:(i + 1) * P, :], zeros[:, :])\
                            .then_inc(zeroed if i else stored, 16)

            def body(g, like):
                for k in range(UNITS):
                    if like >= 1:
                        layer, s = local(g - 1, like - 1)
                        sp_back(sp, layer, s, g - 1, k)
                    if like == -1 and k == 1:
                        zero_padding()
                    if like + 1 < 2 * SEQS:
                        layer, s = local(g + 1, like + 1)
                        sp_front(sp, (g, like), layer, s, g + 1, (like + 1) % 2, k)
                    if layer_at(like) == 1:
                        sp_blocks(sp, (g, like), g - SEQS, like % 2, k)

            over_bodies(sp, body)
            sp.wait_ge(stored, 16 * (2 * SEQS + 2))

        @block.tensor
        def _(pe):
            pe.wait_ge(loaded, N_LOADS)
            pe.wait_ge(prep, PREP_ONES)
            for c in range(CH):
                mm = pe.matmul(side_ps[2][:, 0:DM], one_col[:, c, :], out_w[1][:, c, :], start=(c == 0), stop=(c == CH - 1))
            mm.then_inc(prep_pe, 1)
            pe.wait_ge(prep, PREP_GAIN)
            for c in range(CH):
                mm = pe.matmul(side_ps[2][:, DM:2 * DM], one_col[:, c, :], out_w[1][:, c, :], start=(c == 0), stop=(c == CH - 1))
            mm.then_inc(prep_pe, 1)
            pe.wait_ge(prep, PREP_ALL)

            def body(g, like):
                for k in range(UNITS):
                    pe_core(pe, g, k, like % 2)
                    if like == 2 * SEQS and k > LAST_BACK:
                        return
                    if like >= 1:
                        layer, s = local(g - 1, like - 1)
                        pe_back(pe, (g, like), layer, s, g - 1, (like - 1) % 2, k)
                    if like + 1 < 2 * SEQS:
                        layer, s = local(g + 1, like + 1)
                        pe_front(pe, (g, like), layer, s, g + 1, (like + 1) % 2, k)
                    if layer_at(like) == 1:
                        pe_blocks(pe, (g, like), g - SEQS, k)

            over_bodies(pe, body)

        @block.scalar
        def _(act):
            for dst, name in plain[1::2]:
                act.dma_start(dst[:], T[name]).then_inc(loaded, 16)
            nc.scalar.preload_act_table_set(EXP_LN)
            act.wait_ge(loaded, N_LOADS)
            act.activation(A[0][:, :, :], A[0][:, :, :], ACT.Exp).then_inc(prep_act, 1)
            act.activation(small[:, 0, 0:NS], A[1][:, 0, :], ACT.Abs).then_inc(prep_act, 1)
            act.wait_ge(prep_act, 2)
            act.activation(small[:, 1, 0:NS], small[:, 0, 0:NS], ACT.Exp, scale=-1.0).then_inc(prep_act, 1)
            act.wait_ge(prep_act, 3)
            act.activation(small[:, 3, 0:NS], small[:, 1, 0:NS], ACT.Copy, bias=1.0).then_inc(prep_act, 1)
            act.wait_ge(prep_act, 4)
            act.activation(small[:, 2, 0:NS], small[:, 3, 0:NS], ACT.Ln).then_inc(prep_act, 1)
            act.wait_ge(prep, PREP_ALL)

            def body(g, like):
                for k in range(UNITS):
                    act_core(act, g, k, like % 2, like)
                    if like >= 1:
                        layer, s = local(g - 1, like - 1)
                        act_back(act, (g, like), layer, s, g - 1, (like - 1) % 2, k)
                    if like + 1 < 2 * SEQS:
                        layer, s = local(g + 1, like + 1)
                        act_front(act, (g, like), layer, s, g + 1, (like + 1) % 2, k)
                    if layer_at(like) == 1:
                        act_blocks(act, (g, like), g - SEQS, k)
            over_bodies(act, body)

        @block.vector
        def _(dve):
            step = [0]

            def link(i):
                step[0] += 1
                i.then_inc(prep, 1)
                dve.wait_ge(prep, step[0])

            link(dve.memset(zeros[:, :], 0.0))
            dve.wait_ge(loaded, N_LOADS)
            link(dve.memset(one_col[:, :, :], 0.0))
            for c in range(CH):
                link(dve.tensor_scalar(one_col[:, c, :], one_col[:, c, :], ln_b[:, c:c + 1], None, ALU.add))
            assert step[0] == PREP_ONES
            dve.wait_ge(prep_pe, 1)
            for c in range(CH):
                link(dve.tensor_scalar(out_w[1][:, c, :], out_w[1][:, c, :], ln_g[:, c:c + 1], None, ALU.mult))
            link(dve.memset(one_col[:, :, :], 1.0))
            assert step[0] == PREP_GAIN
            dve.wait_ge(prep_pe, 2)
            link(dve.tensor_copy(bias_out[:, :], side_ps[2][:, 0:DM]))
            link(dve.tensor_copy(gain_sum[:, :], side_ps[2][:, DM:2 * DM]))
            link(dve.memset(ones_e[:, :], 1.0))
            link(dve.memset(idle[:, :], 0.0))
            link(dve.memset(probs[:, :, :], SENTINEL))
            link(dve.memset(wanted[:, :, :], SENTINEL))
            link(dve.memset(conv_in[:, :, 0:TAPS - 1], 0.0))
            link(dve.tensor_copy(spread[:, :, :], part_rows[:, :].unsqueeze(2).to_broadcast([96, 2 * NS, P])))
            dve.wait_ge(prep_act, 5)
            link(dve.tensor_scalar(A[0][:, :, :], A[0][:, :, :], -1.0, None, ALU.mult))
            link(dve.scalar_tensor_tensor(small[:, 3, 0:NS], small[:, 3, 0:NS], -1.0, small[:, 1, 0:NS], ALU.add,
                                          ALU.subtract))
            link(dve.tensor_tensor(small[:, 3, 0:NS], small[:, 2, 0:NS], small[:, 3, 0:NS], ALU.subtract))
            link(dve.scalar_tensor_tensor(small[:, 3, 0:NS], A[1][:, 0, :], 0.0, small[:, 3, 0:NS], ALU.max, ALU.add))
            for c in range(CH):
                link(dve.tensor_scalar(A[1][:, c, :], small[:, 3, 0:NS], -1.0, None, ALU.mult))
            assert step[0] == PREP_ALL, step[0]

            def body(g, like):
                for k in range(UNITS):
                    dve_core(dve, g, k, like % 2)
                    if like >= 1 and k == R_LAG:
                        dve_take_y(dve, g - 1, 1, (like - 1) % 2, int(like - 1 >= SEQS))
                    if layer_at(like - 1) == 0 and k == R_LAG + 1:
                        dve_gate_y(dve, g - 1, 1, (like - 1) % 2)
                    if layer_at(like) == 0 and k == NS + R_LAG + 1:
                        dve_gate_y(dve, g, 0, like % 2)
                    if 0 <= like < 2 * SEQS and k == NS + R_LAG:
                        dve_take_y(dve, g, 0, like % 2, int(like >= SEQS))
                    if like >= 1:
                        layer, s = local(g - 1, like - 1)
                        dve_back(dve, (g, like), layer, s, g - 1, (like - 1) % 2, k)
                    if like == 2 * SEQS and k > LAST_BACK:
                        return
                    if like + 1 < 2 * SEQS:
                        layer, s = local(g + 1, like + 1)
                        dve_front(dve, (g, like), layer, s, g + 1, (like + 1) % 2, k)
                    if layer_at(like) == 1:
                        dve_blocks(dve, (g, like), g - SEQS, k)

            over_bodies(dve, body)

        @block.gpsimd
        def _(pool):
            def body(g, like):
                for k in range(UNITS):
                    front = g + 1 - SEQS if layer_at(like + 1) == 1 else None
                    back = g - 1 - SEQS if layer_at(like - 1) == 1 else None
                    pool_waits(pool, front, back, k)
                    if 0 <= like < 2 * SEQS:
                        pool_core(pool, g, k)
                    if layer_at(like - 1) is not None:
                        layer, s = local(g - 1, like - 1)
                        pool_back(pool, (g, like), layer, s, g - 1, k)
                    if 0 <= like < 2 * SEQS and k == 1:
                        pool_u(pool, g, like % 2)
                    pool_indirect(pool, front, back, (like + 1) % 2, k)

            over_bodies(pool, body)


PREP_ZERO = 1
PREP_ONES = PREP_ZERO + 1 + CH
PREP_GAIN = PREP_ONES + CH + 1
PREP_ALL = PREP_GAIN + 8 + 4 + CH


def kernel(**inputs):
    import ml_dtypes
    import numpy as np
    import concourse.bacc as bacc
    from concourse.bass_utils import run_bass_kernel_spmd

    w = {k: np.asarray(v) for k, v in inputs.items()}

    def halves(a):
        return a.reshape((CH, P) + a.shape[1:]).swapaxes(0, 1)

    data = {
        "x": w["L0_attn_hidden_states"].reshape(SEQS * LEN, DM),
        "ident": np.eye(P, dtype=np.float32),
        "part_rows": np.tile(np.eye(2 * NS, dtype=np.float32), (3, 1)),
        "in_w": w["L0_attn_in_proj_w"].T,
        "conv_w0": halves(w["L0_attn_conv_w"]),
        "conv_b0": halves(w["L0_attn_conv_b"]),
        "x_w": halves(w["L0_attn_x_proj_w"].T),
        "dt_w": w["L0_attn_dt_proj_w"].T,
        "dt_b0": halves(w["L0_attn_dt_proj_b"]),
        "A_log0": halves(w["L0_attn_A_log"]),
        "skip_d": halves(w["L0_attn_D"]),
        "out_w0": halves(w["L0_attn_out_proj_w"].T),
        "sel_w": w["L0_ffn_expert_sel"].T,
        "keys": w["L0_ffn_keys"].transpose(1, 0, 2).reshape(DM, E0 * EH),
        "values": w["L0_ffn_values"].reshape(4, P, DM).transpose(1, 0, 2),
        "route": w["L0_ffn_route_scale"],
        "side_w": np.concatenate([w["L1_attn_W_left"].T, w["L1_attn_W_right"].T], axis=1),
        "conv_w1": halves(w["L1_attn_conv_w"][:, 0, :]),
        "conv_b1": halves(w["L1_attn_conv_b"]),
        "delta_w": halves(w["L1_attn_W_delta"].T),
        "dt_b1": halves(w["L1_attn_b_delta"]),
        "bc_w": halves(np.concatenate([w["L1_attn_W_B"], w["L1_attn_W_C"]], axis=0).T),
        "A_log1": w["L1_attn_A_log"],
        "ln_g": halves(w["L1_attn_ln_g"]),
        "ln_b": halves(w["L1_attn_ln_b"]),
        "out_w1": halves(w["L1_attn_W_out"].T),
        "gate_w": w["L1_ffn_gate_w"].T,
        "gate_b": w["L1_ffn_gate_b"],
        "expert_bias": w["L1_ffn_expert_bias"],
        "experts": np.concatenate([
            w["L1_ffn_w1"],
            w["L1_ffn_w2"].reshape(E1, FB, P, DM).transpose(0, 2, 1, 3).reshape(E1, P, FF),
            w["L1_ffn_b1"].reshape(E1, FB, P).transpose(0, 2, 1),
            np.broadcast_to(w["L1_ffn_b2"][:, None, :], (E1, P, DM))], axis=2),
        "before": np.triu(np.ones((P, P), np.float32), 1).astype(ml_dtypes.bfloat16),
        "ones": np.ones((P, P), ml_dtypes.bfloat16),
        "tile_sizes": np.tile(np.arange(E1, dtype=np.float32) * P, E1),
        "tile_numbers": np.repeat(np.arange(BLOCKS, dtype=np.float32), E1),
    }
    nc = bacc.Bacc("TRN2", target_bir_lowering=False, num_devices=1)
    arrays, T = {}, {}
    for name, a in data.items():
        arrays[f"in_{name}"] = np.ascontiguousarray(a)
        T[name] = nc.dram_tensor(f"in_{name}", a.shape, mybir.dt.from_np(a.dtype), kind="ExternalInput").ap()
    T["x1"] = nc.dram_tensor("x1", (SEQS * LEN, DM), F32, kind="Internal").ap()
    for j in range(2):
        T[f"sorted_x{j}"] = nc.dram_tensor(f"sorted_x{j}", (BLOCKS * P, DM), F32, kind="Internal").ap()
        T[f"sorted_y{j}"] = nc.dram_tensor(f"sorted_y{j}", (BLOCKS * P, DM), F32, kind="Internal").ap()
    out = nc.dram_tensor("out_x", (SEQS * LEN, DM), F32, kind="ExternalOutput").ap()
    build(nc, T, out)
    r = run_bass_kernel_spmd(nc, [arrays], core_ids=[0])
    return r.results[0]["out_x"].reshape(SEQS, LEN, DM)
```
